# Optimizing a Trainium2 kernel written in Bass

```python
import numpy as np
import jax
import jax.numpy as jnp

def _softmax(x, axis=-1):
    return jax.nn.softmax(x, axis=axis)

def _gelu(x):
    return jax.nn.gelu(x, approximate=True)

def _silu(x):
    return jax.nn.silu(x)

def _sigmoid(x):
    return jax.nn.sigmoid(x)

def _layernorm(x, axis=-1, eps=1e-05):
    m = jnp.mean(x, axis=axis, keepdims=True)
    v = jnp.var(x, axis=axis, keepdims=True)
    return (x - m) / jnp.sqrt(v + eps)

def _scatter_add(tgt, idx, src, axis=0):
    return tgt.at[idx].add(src)

def _segment_sum(src, seg, n):
    return jax.ops.segment_sum(src, seg, n)
kernel_name = 'mk_macaron_d1_jaxref_r8_aafb87'

def setup_inputs(seed: int=0):
    np.random.seed(seed)
    _w = jnp.asarray

    def _L0_attn_setup():
        import jax, jax.numpy as jnp
        import numpy as np
        B, T, V = (4, 512, 128)
        DECAY_INIT = 3.0
        key = jax.random.key(seed)
        k_x, = jax.random.split(key, 1)
        x = jax.random.normal(k_x, (B, T, V), dtype=jnp.float32)
        return {'x': x, 'decay_logit': jnp.asarray(DECAY_INIT, dtype=jnp.float32), 'out_scale': jnp.asarray(0.1, dtype=jnp.float32), 'q_scale': jnp.ones((V,), dtype=jnp.float32), 'k_scale': jnp.ones((V,), dtype=jnp.float32)}
    _L0_attn_in = _L0_attn_setup()

    def _L0_ffn_setup():
        import jax, jax.numpy as jnp
        import numpy as np
        B, S, H, D, E = (4, 128, 128, 512, 8)
        key = jax.random.key(seed)
        ks = jax.random.split(key, 12)

        def init(k, shape, fan_in):
            return jax.random.normal(k, shape, jnp.float32) / np.float32(np.sqrt(fan_in))
        return {'x': jax.random.normal(ks[0], (B, S, H), jnp.float32), 'Wq': init(ks[1], (H, H), H), 'bq': jnp.zeros((H,), jnp.float32), 'Wk': init(ks[2], (H, H), H), 'bk': jnp.zeros((H,), jnp.float32), 'Wv': init(ks[3], (H, H), H), 'bv': jnp.zeros((H,), jnp.float32), 'Wo': init(ks[4], (H, H), H), 'bo': jnp.zeros((H,), jnp.float32), 'Wg': init(ks[5], (H, E), H), 'bg': jnp.zeros((E,), jnp.float32), 'W1': init(ks[6], (E, H, D), H), 'b1': jnp.zeros((E, D), jnp.float32), 'W2': init(ks[7], (E, D, H), D), 'b2': jnp.zeros((E, H), jnp.float32)}
    _L0_ffn_in = _L0_ffn_setup()
    _d = {'L0_attn_x': _L0_attn_in['x'], 'L0_attn_decay_logit': _L0_attn_in['decay_logit'], 'L0_attn_out_scale': _L0_attn_in['out_scale'], 'L0_attn_q_scale': _L0_attn_in['q_scale'], 'L0_attn_k_scale': _L0_attn_in['k_scale'], 'L0_ffn_Wq': _L0_ffn_in['Wq'], 'L0_ffn_bq': _L0_ffn_in['bq'], 'L0_ffn_Wk': _L0_ffn_in['Wk'], 'L0_ffn_bk': _L0_ffn_in['bk'], 'L0_ffn_Wv': _L0_ffn_in['Wv'], 'L0_ffn_bv': _L0_ffn_in['bv'], 'L0_ffn_Wo': _L0_ffn_in['Wo'], 'L0_ffn_bo': _L0_ffn_in['bo'], 'L0_ffn_Wg': _L0_ffn_in['Wg'], 'L0_ffn_bg': _L0_ffn_in['bg'], 'L0_ffn_W1': _L0_ffn_in['W1'], 'L0_ffn_b1': _L0_ffn_in['b1'], 'L0_ffn_W2': _L0_ffn_in['W2'], 'L0_ffn_b2': _L0_ffn_in['b2']}
    _x0 = _d['L0_attn_x']
    _d['L0_attn_x'] = jax.random.normal(jax.random.fold_in(jax.random.key(seed), 1), (8, 256, 128), dtype=_x0.dtype)
    del _x0
    return _d

def reference(L0_attn_x, L0_attn_decay_logit, L0_attn_out_scale, L0_attn_q_scale, L0_attn_k_scale, L0_ffn_Wq, L0_ffn_bq, L0_ffn_Wk, L0_ffn_bk, L0_ffn_Wv, L0_ffn_bv, L0_ffn_Wo, L0_ffn_bo, L0_ffn_Wg, L0_ffn_bg, L0_ffn_W1, L0_ffn_b1, L0_ffn_W2, L0_ffn_b2):

    def _L0_attn_ref(x, decay_logit, out_scale, q_scale, k_scale):
        import jax, jax.numpy as jnp
        import numpy as np
        B, T, V = (4, 512, 128)
        DECAY_INIT = 3.0
        dtype = x.dtype
        Bx, Tx, Vx = x.shape
        queries = x * q_scale.astype(dtype)
        keys = x * k_scale.astype(dtype)
        scores = jnp.einsum('btv,bsv->bts', queries, keys)
        decay = jax.nn.sigmoid(decay_logit)
        pos = jnp.arange(Tx)
        diff = pos[None, :] - pos[:, None]
        causal = diff > 0
        weights = decay ** jnp.maximum(diff.astype(jnp.float32) - 1.0, 0.0) * causal
        scores = scores * weights.astype(dtype)[None]
        retrieved = jnp.einsum('bts,bsv->btv', scores, x)
        return retrieved * out_scale.astype(dtype)

    def _L0_ffn_ref(x, Wq, bq, Wk, bk, Wv, bv, Wo, bo, Wg, bg, W1, b1, W2, b2):
        import jax, jax.numpy as jnp
        import numpy as np
        B, S, H, D, E = (4, 128, 128, 512, 8)
        q = x @ Wq + bq
        k = x @ Wk + bk
        v = x @ Wv + bv
        scale = jnp.asarray(1.0 / np.sqrt(H), x.dtype)
        scores = jnp.einsum('bqh,bkh->bqk', q, k) * scale
        attn = jax.nn.softmax(scores, axis=-1)
        a = jnp.einsum('bqk,bkh->bqh', attn, v) @ Wo + bo
        x = x + a
        gates = jax.nn.softmax(x @ Wg + bg, axis=-1)
        hmid = jax.nn.relu(jnp.einsum('bsh,ehd->bsed', x, W1) + b1)
        eout = jnp.einsum('bsed,edh->bseh', hmid, W2) + b2
        y = jnp.einsum('bse,bseh->bsh', gates, eout)
        return x + y
    x = L0_attn_x
    x = x + 0.5 * _L0_ffn_ref(_layernorm(x, axis=-1), L0_ffn_Wq, L0_ffn_bq, L0_ffn_Wk, L0_ffn_bk, L0_ffn_Wv, L0_ffn_bv, L0_ffn_Wo, L0_ffn_bo, L0_ffn_Wg, L0_ffn_bg, L0_ffn_W1, L0_ffn_b1, L0_ffn_W2, L0_ffn_b2)
    x = x + _L0_attn_ref(_layernorm(x, axis=-1), L0_attn_decay_logit, L0_attn_out_scale, L0_attn_q_scale, L0_attn_k_scale)
    x = x + 0.5 * _L0_ffn_ref(_layernorm(x, axis=-1), L0_ffn_Wq, L0_ffn_bq, L0_ffn_Wk, L0_ffn_bk, L0_ffn_Wv, L0_ffn_bv, L0_ffn_Wo, L0_ffn_bo, L0_ffn_Wg, L0_ffn_bg, L0_ffn_W1, L0_ffn_b1, L0_ffn_W2, L0_ffn_b2)
    return x

_drawn_inputs = setup_inputs


def setup_inputs(seed=0):
    import zlib

    import numpy as np

    out = dict(_drawn_inputs(seed))
    spreads = {'L0_attn_q_scale': (1.0, 0.2),
     'L0_attn_k_scale': (1.0, 0.2),
     'L0_ffn_bq': (0.0, 0.8),
     'L0_ffn_bk': (0.0, 0.8),
     'L0_ffn_bv': (0.0, 0.1),
     'L0_ffn_bo': (0.0, 0.1),
     'L0_ffn_bg': (0.0, 0.779),
     'L0_ffn_b1': (0.0, 0.406),
     'L0_ffn_b2': (0.0, 0.278)}
    factors = {}
    for name, (base, spread) in spreads.items():
        noise = np.random.default_rng([zlib.crc32(name.encode()), seed]).standard_normal(out[name].shape)
        drawn = base * np.exp(spread * noise) if base else spread * noise
        out[name] = jnp.asarray(drawn.astype(out[name].dtype))
    for name, factor in factors.items():
        out[name] = (out[name] * factor).astype(out[name].dtype)
    return out
```

```python
from contextlib import ExitStack

import concourse.bass as bass
from concourse import mybir

F32 = mybir.dt.float32
F32R = mybir.dt.float32r
ALU = mybir.AluOpType
ACT = mybir.ActivationFunctionType
AX_X = mybir.AxisListType.X

P = 128
NCH = 4
CH = 512
TL = CH // P
SEQ = 256
NB = CH // SEQ
NE = 8
DQ = 4
UNITS = NE * DQ
PHASES = 2 * NCH
EPS = 1e-5

LAG = 3
NU = 2
NWR = 4
NHF = 4
NHS = 4

ROW_B1, ROW_B2 = 0, 32
ROW_BQ, ROW_BK, ROW_BV, ROW_BO, ROW_QS, ROW_KS = range(40, 46)
NROWS = 46

AT_NORM = 0
AT_UT, AT_Q, AT_K = 5, 7, 8
AT_SC = (9, 10)
AT_AT = (13, 15)
AT_C, AT_A, AT_LG, AT_GT = 17, 19, 22, 26
AT_FOLD = 7
AT_RNORM = 8
AT_VT = 12
AT_RSC = (14, 16)
AT_R = 19

HI_ON_ACT = [n % 2 == 0 for n in range(UNITS)]


def macaron(nc, x, decay_logit, out_scale, q_scale, k_scale, Wq, bq, Wk, bk, Wv, bv, Wo, bo,
            Wg, bg, W1, b1, W2, b2, shapes, gates_dram, out):
    ctx = ExitStack()
    with ctx:
        def sb(name, shape, dt=F32):
            return ctx.enter_context(nc.sbuf_tensor(name, shape, dt))

        def bank(name):
            return ctx.enter_context(nc.psum_tensor(name, [P, 512], F32))

        def sem(name):
            return ctx.enter_context(nc.semaphore(name))

        xs = sb("xs", [P, NCH * TL, P])
        w1raw = sb("w1raw", [P, NWR, CH])
        w2raw = sb("w2raw", [P, NWR, CH])
        w1hi = sb("w1hi", [P, NE, CH], F32R)
        w1lo = sb("w1lo", [P, NE, CH], F32R)
        w2hi = sb("w2hi", [P, NE, CH], F32R)
        w2lo = sb("w2lo", [P, NE, CH], F32R)
        wq = sb("wq", [P, P])
        wk = sb("wk", [P, P])
        wv = sb("wv", [P, P])
        wo = sb("wo", [P, P])
        wvT = sb("wvT", [P, P])
        wvo = sb("wvo", [P, P])
        bvo = sb("bvo", [P, 1])
        wg = sb("wg", [P, NE])
        bg_all = sb("bg_all", [P, NE])
        prow = sb("prow", [NROWS, P])
        pcol = sb("pcol", [P, NROWS])
        shp = sb("shp", [P, P + 2 * 384])
        ident = shp[:, 0:P]
        expo = shp[:, P:P + 384]
        causal = shp[:, P + 384:P + 768]
        dcy = sb("dcy", [P, 8])
        oscale = sb("oscale", [P, 1])
        dmask = sb("dmask", [P, 384])
        mhalf = sb("mhalf", [P, TL])
        u = sb("u", [P, TL, P])
        v = sb("v", [P, TL, P])
        st_p = sb("st_p", [P, TL, 6])
        mv_p = sb("mv_p", [P, TL, 2])
        rs_p = sb("rs_p", [P, 2, TL])
        st_r = sb("st_r", [P, TL, 6])
        mv_r = sb("mv_r", [P, TL, 2])
        rs_r = sb("rs_r", [P, 2, TL])
        uT = sb("uT", [P, CH])
        qT = sb("qT", [P, CH])
        kT = sb("kT", [P, CH])
        smx = sb("smx", [P, NB, 2])
        nmx = sb("nmx", [P, NB, 2])
        esum = sb("esum", [P, NB, 2])
        rsum = sb("rsum", [P, NB, 2])
        ex = sb("ex", [P, NB, 2, SEQ])
        attn = sb("attn", [P, NB, 2, SEQ])
        attnT = sb("attnT", [P, NB, 2, SEQ])
        cT = sb("cT", [P, CH])
        facc = sb("facc", [P, 2, CH])
        zhi = sb("zhi", [P, 2, CH], F32R)
        zlo = sb("zlo", [P, 2, CH], F32R)
        lg = sb("lg", [P, TL, NE])
        lmx = sb("lmx", [P, TL])
        lsh = sb("lsh", [P, TL, NE])
        lex = sb("lex", [P, TL, NE])
        lsm = sb("lsm", [P, TL])
        lrc = sb("lrc", [P, TL])
        gts = sb("gts", [P, TL, NE])
        gT = sb("gT", [NE, CH])
        gbc = sb("gbc", [P, 2, NE, CH])
        hF = sb("hF", [P, NHF, CH])
        hhi = sb("hhi", [P, NHS, CH], F32R)
        hlo = sb("hlo", [P, NHS, CH], F32R)
        gated = sb("gated", [P, 2, CH])
        rqT = sb("rqT", [P, CH])
        rkT = sb("rkT", [P, CH])
        pT = sb("pT", [P, NB, 384])

        up_ps = [bank(f"up_ps{i}") for i in range(NU)]
        down_ps = [bank(f"down_ps{i}") for i in range(2)]
        p_ps = [bank(f"p_ps{i}") for i in range(2)]
        r_ps = [bank(f"r_ps{i}") for i in range(2)]

        shapes_in = sem("shapes_in")
        x0_in = sem("x0_in")
        xrest_in = sem("xrest_in")
        prow_in = sem("prow_in")
        wattn_in = sem("wattn_in")
        bcast_in = sem("bcast_in")
        w1_in = [sem(f"w1_in{e}") for e in range(NE)]
        w2_in = [sem(f"w2_in{e}") for e in range(NE)]
        mhalf_set = sem("mhalf_set")
        whi_done = sem("whi_done")
        wlo_done = sem("wlo_done")
        pcolT_ready, pcol_done = sem("pcolT_ready"), sem("pcol_done")
        wvT_ready, wvT_done = sem("wvT_ready"), sem("wvT_done")
        wvo_ready, wvo_done = sem("wvo_ready"), sem("wvo_done")
        bvo_ready, bvo_done = sem("bvo_ready"), sem("bvo_done")
        dcy_vec, dcy_act, dmask_done = sem("dcy_vec"), sem("dcy_act"), sem("dmask_done")
        up_ready, relu_done = sem("up_ready"), sem("relu_done")
        hi_act_done, hi_vec_done, lo_done = sem("hi_act_done"), sem("hi_vec_done"), sem("lo_done")
        down_ready, gate_done, sum_done = sem("down_ready"), sem("gate_done"), sem("sum_done")
        p_stat, p_var, p_eps, p_rstd, p_u = (sem(f"p_{n}") for n in ("stat", "var", "eps", "rstd", "u"))
        r_stat, r_var, r_eps, r_rstd, r_v = (sem(f"r_{n}") for n in ("stat", "var", "eps", "rstd", "v"))
        uT_ready, uT_done = sem("uT_ready"), sem("uT_done")
        q_ready, q_done = sem("q_ready"), sem("q_done")
        k_ready, k_done = sem("k_ready"), sem("k_done")
        sc_ready, smx_done, nmx_done = sem("sc_ready"), sem("smx_done"), sem("nmx_done")
        exp_done, rsum_done, attn_done = sem("exp_done"), sem("rsum_done"), sem("attn_done")
        at_ready, at_done = sem("at_ready"), sem("at_done")
        c_ready, c_done = sem("c_ready"), sem("c_done")
        a_ready, z_done, zhi_done, zlo_done = sem("a_ready"), sem("z_done"), sem("zhi_done"), sem("zlo_done")
        lg_ready, lg_done, lmx_done, lsh_done = sem("lg_ready"), sem("lg_done"), sem("lmx_done"), sem("lsh_done")
        lex_done, lsm_done, lrc_done, gts_done = sem("lex_done"), sem("lsm_done"), sem("lrc_done"), sem("gts_done")
        gT_ready, gT_done = sem("gT_ready"), sem("gT_done")
        gates_out = sem("gates_out")
        gbc_in = [sem(f"gbc_in{i}") for i in range(2)]
        fold_ready, fold_done = sem("fold_ready"), sem("fold_done")
        vT_ready, rqk_done = sem("vT_ready"), sem("rqk_done")
        rsc_ready, pT_done = sem("rsc_ready"), sem("pT_done")
        r_ready, rx_done = sem("r_ready"), sem("rx_done")
        stored = sem("stored")

        per_phase = {True: HI_ON_ACT.count(True), False: HI_ON_ACT.count(False)}

        def hi_count(j, n, on_act):
            return per_phase[on_act] * j + HI_ON_ACT[:n + 1].count(on_act)

        def rows_of(chunk):
            return xs[:, bass.ds(chunk * TL, TL), :] if not isinstance(chunk, int) else \
                xs[:, chunk * TL:(chunk + 1) * TL, :]

        def row_tile(chunk, t):
            return xs[:, bass.ds(chunk * TL + t, 1), :] if not isinstance(chunk, int) else \
                xs[:, chunk * TL + t, :]

        def dram_rows(t, chunk0, n):
            return t.rearrange("b s h -> (b s) h").rearrange("(t p) h -> p t h", p=P)[
                :, chunk0 * TL:(chunk0 + n) * TL, :]

        block = ctx.enter_context(nc.Block())

        @block.sync
        def _(sp):
            sp.dma_start(rows_of(0), dram_rows(x, 0, 1)).then_inc(x0_in, 16)
            sp.dma_start(shp[:, :], shapes).then_inc(shapes_in, 16)
            for w, dst in ((Wq, wq), (Wk, wk), (Wv, wv), (Wo, wo), (Wg, wg)):
                sp.dma_start(dst[:, :], w).then_inc(wattn_in, 16)
            def load_expert(e):
                if e >= NWR:
                    sp.wait_ge(wlo_done, 2 * (e - NWR) + 1)
                sp.dma_start(w1raw[:, e % NWR, :], W1[e]).then_inc(w1_in[e], 16)
                if e >= NWR:
                    sp.wait_ge(wlo_done, 2 * (e - NWR) + 2)
                sp.dma_start(w2raw[:, e % NWR, :].rearrange("p (c h) -> p c h", c=DQ),
                             W2[e].rearrange("(c p) h -> p c h", p=P)).then_inc(w2_in[e], 16)

            def spread_gates(k):
                par = k % 2
                sp.wait_ge(gT_done, k + 1)
                if k >= 2:
                    sp.wait_ge(gbc_in[par], 16 * (k // 2))
                sp.dma_start(gates_dram[par], gT[:, :]).then_inc(gates_out, 16)
                sp.wait_ge(gates_out, 16 * (k + 1))
                if k >= 2:
                    sp.wait_ge(gate_done, NE * (k - 1))
                sp.dma_start(gbc[:, par, :, :], gates_dram[par:par + 1].to_broadcast([P, NE, CH])
                             ).then_inc(gbc_in[par], 16)

            def store(j):
                c = j % NCH
                sp.wait_ge(fold_done, j + 1)
                sp.dma_start(dram_rows(out, c, 1), rows_of(c)).then_inc(stored, 16)

            for e in range(NWR):
                load_expert(e)
            spread_gates(0)
            for e in range(NWR, NE):
                load_expert(e)
            for j in range(PHASES):
                if j > NCH:
                    store(j - 1)
                if j + 1 < PHASES:
                    spread_gates(j + 1)
            store(PHASES - 1)
            sp.wait_ge(stored, 16 * NCH)

        @block.tensor
        def _(pe):
            def up(j, n):
                e, d = divmod(n, DQ)
                T = UNITS * j + n
                if n == 0:
                    pe.wait_ge(zlo_done, j + 1)
                if j == 0 and d == 0:
                    pe.wait_ge(wlo_done, 2 * e + 1)
                if T >= NU:
                    pe.wait_ge(relu_done, T - NU + 1)
                dst = up_ps[n % NU][:, :]
                cols = slice(P * d, P * d + P)
                pe.matmul(dst, w1lo[:, e, cols], zhi[:, j % 2, :], start=True, stop=False)
                pe.matmul(dst, w1hi[:, e, cols], zlo[:, j % 2, :], start=False, stop=False)
                pe.matmul(dst, w1hi[:, e, cols], zhi[:, j % 2, :], start=False, stop=True).then_inc(up_ready, 1)

            def down(j, n):
                e, d = divmod(n, DQ)
                T = UNITS * j + n
                if j == 0 and d == 0:
                    pe.wait_ge(wlo_done, 2 * e + 2)
                G = NE * j + e
                if d == 0 and G >= 2:
                    pe.wait_ge(gate_done, G - 1)
                pe.wait_ge(lo_done, T + 1)
                dst = down_ps[e % 2][:, :]
                cols = slice(P * d, P * d + P)
                h = T % NHS
                pe.matmul(dst, w2lo[:, e, cols], hhi[:, h, :], start=(d == 0), stop=False)
                pe.matmul(dst, w2hi[:, e, cols], hlo[:, h, :], start=False, stop=False)
                pe.matmul(dst, w2hi[:, e, cols], hhi[:, h, :], start=False, stop=(d == DQ - 1)
                          ).then_inc(down_ready, 1)

            def transpose_tiles(dst, src_of, done):
                for t in range(TL):
                    last = pe.transpose(dst[:, t * P:(t + 1) * P], src_of(t), ident)
                last.then_inc(done, 1)

            def p_uT(k):
                pe.wait_ge(p_u, k + 1)
                if k >= 1:
                    pe.wait_ge(gT_done, k)
                transpose_tiles(p_ps[0], lambda t: u[:, t, :], uT_ready)

            def p_q(k):
                pe.wait_ge(uT_done, k + 1)
                pe.matmul(p_ps[1][:, :], wq[:, :], uT[:, :], start=True, stop=True).then_inc(q_ready, 1)

            def p_k(k):
                pe.wait_ge(uT_done, k + 1)
                pe.matmul(p_ps[0][:, :], wk[:, :], uT[:, :], start=True, stop=True).then_inc(k_ready, 1)

            def p_scores(k, b):
                pe.wait_ge(q_done, k + 1)
                pe.wait_ge(k_done, k + 1)
                keys = kT[:, b * SEQ:(b + 1) * SEQ]
                for i in range(2):
                    last = pe.matmul(p_ps[1 - b][:, i * SEQ:(i + 1) * SEQ],
                                     qT[:, b * SEQ + i * P:b * SEQ + (i + 1) * P], keys, start=True, stop=True)
                last.then_inc(sc_ready, 1)

            def p_attnT(k, b):
                pe.wait_ge(attn_done, NB * k + b + 1)
                for kt in range(2):
                    for i in range(2):
                        at = kt * SEQ + i * P
                        last = pe.transpose(p_ps[1 - b][:, at:at + P], attn[:, b, i, kt * P:(kt + 1) * P], ident)
                last.then_inc(at_ready, 1)

            def p_context(k):
                pe.wait_ge(at_done, NB * (k + 1))
                for b in range(NB):
                    for kt in range(2):
                        last = pe.matmul(p_ps[1][:, b * SEQ:(b + 1) * SEQ], u[:, 2 * b + kt, :],
                                         attnT[:, b, kt, :], start=(kt == 0), stop=(kt == 1))
                last.then_inc(c_ready, 1)

            def p_project(k):
                pe.wait_ge(c_done, k + 1)
                if k == 0:
                    pe.wait_ge(wvo_done, 1)
                pe.matmul(p_ps[0][:, :], wvo[:, :], cT[:, :], start=True, stop=True).then_inc(a_ready, 1)

            def p_logits(k):
                pe.wait_ge(z_done, k + 1)
                for t in range(TL):
                    last = pe.matmul(p_ps[1][:, t * NE:(t + 1) * NE], facc[:, k % 2, t * P:(t + 1) * P],
                                     wg[:, :], start=True, stop=True)
                last.then_inc(lg_ready, 1)

            def p_gatesT(k):
                pe.wait_ge(gts_done, k + 1)
                for t in range(TL):
                    last = pe.transpose(p_ps[0][0:NE, t * P:(t + 1) * P], gts[:, t, :], ident)
                last.then_inc(gT_ready, 1)

            def fold(j):
                pe.wait_ge(sum_done, NE * (j + 1))
                if 1 <= j <= NCH:
                    pe.wait_ge(rx_done, j)
                elif j > NCH:
                    pe.wait_ge(fold_done, j)
                transpose_tiles(r_ps[0], lambda t: facc[:, j % 2, t * P:(t + 1) * P], fold_ready)

            def r_vT(c):
                pe.wait_ge(r_v, c + 1)
                transpose_tiles(r_ps[1], lambda t: v[:, t, :], vT_ready)

            def r_scores(c, b):
                pe.wait_ge(rqk_done, c + 1)
                o = b * SEQ
                pe.matmul(r_ps[b][:, 0:P], rkT[:, o:o + P], rqT[:, o:o + P], start=True, stop=True)
                pe.matmul(r_ps[b][:, P:P + SEQ], rkT[:, o + P:o + SEQ], rqT[:, o:o + SEQ],
                          start=True, stop=True).then_inc(rsc_ready, 1)

            def r_retrieve(c):
                pe.wait_ge(pT_done, NB * (c + 1))
                for b in range(NB):
                    t0 = r_ps[0][:, (2 * b) * P:(2 * b + 1) * P]
                    t1 = r_ps[0][:, (2 * b + 1) * P:(2 * b + 2) * P]
                    pe.matmul(t0, pT[:, b, 0:P], v[:, 2 * b, :], start=True, stop=False)
                    pe.matmul(t0, pT[:, b, P:2 * P], v[:, 2 * b + 1, :], start=False, stop=True)
                    last = pe.matmul(t1, pT[:, b, 2 * P:3 * P], v[:, 2 * b + 1, :], start=True, stop=True)
                last.then_inc(r_ready, 1)

            pe.wait_ge(shapes_in, 16)
            p_uT(0)
            pe.wait_ge(wattn_in, 16 * 5)
            p_q(0)
            p_k(0)
            pe.wait_ge(prow_in, 16 * 8)
            pe.transpose(up_ps[0][:, 0:NROWS], prow[:, :], ident[0:NROWS, 0:NROWS]).then_inc(pcolT_ready, 1)
            pe.transpose(up_ps[1][:, 0:P], wv[:, :], ident).then_inc(wvT_ready, 1)
            pe.wait_ge(wvT_done, 1)
            pe.matmul(down_ps[0][:, 0:P], wvT[:, :], wo[:, :], start=True, stop=True).then_inc(wvo_ready, 1)
            pe.wait_ge(pcol_done, 1)
            pe.matmul(down_ps[1][:, 0:1], wo[:, :], pcol[:, ROW_BV:ROW_BV + 1], start=True, stop=True
                      ).then_inc(bvo_ready, 1)
            for b in range(NB):
                p_scores(0, b)
            for b in range(NB):
                p_attnT(0, b)
            p_context(0)
            p_project(0)
            p_logits(0)
            p_gatesT(0)
            pe.wait_ge(wvo_done, 1)
            pe.wait_ge(bvo_done, 1)

            for j in range(PHASES):
                for n in range(UNITS):
                    up(j, n)
                    if n >= LAG:
                        down(j, n - LAG)
                    elif j >= 1:
                        down(j - 1, UNITS + n - LAG)
                    if j >= 1:
                        if n == AT_FOLD:
                            fold(j - 1)
                        if j <= NCH:
                            if n == AT_VT:
                                r_vT(j - 1)
                            if n in AT_RSC:
                                r_scores(j - 1, AT_RSC.index(n))
                            if n == AT_R:
                                r_retrieve(j - 1)
                    k = j + 1
                    if k < PHASES:
                        if n == AT_UT:
                            p_uT(k)
                        if n == AT_Q:
                            p_q(k)
                        if n == AT_K:
                            p_k(k)
                        if n in AT_SC:
                            p_scores(k, AT_SC.index(n))
                        if n in AT_AT:
                            p_attnT(k, AT_AT.index(n))
                        if n == AT_C:
                            p_context(k)
                        if n == AT_A:
                            p_project(k)
                        if n == AT_LG:
                            p_logits(k)
                        if n == AT_GT:
                            p_gatesT(k)
            for n in range(UNITS - LAG, UNITS):
                down(PHASES - 1, n)
            fold(PHASES - 1)

        @block.scalar
        def _(act):
            for row, src in ((ROW_B1, b1.rearrange("e (c d) -> (e c) d", c=DQ)), (ROW_B2, b2)):
                act.dma_start(prow[row:row + src.shape[0], :], src).then_inc(prow_in, 16)
            for row, src in ((ROW_BQ, bq), (ROW_BK, bk), (ROW_BV, bv), (ROW_BO, bo),
                             (ROW_QS, q_scale), (ROW_KS, k_scale)):
                act.dma_start(prow[row:row + 1, :], src.rearrange("(a h) -> a h", a=1)).then_inc(prow_in, 16)
            act.dma_start(bg_all[:, :], bg.rearrange("(a e) -> a e", a=1).to_broadcast([P, NE])).then_inc(bcast_in, 16)
            act.dma_start(dcy[:, 0:1], decay_logit.to_broadcast([P, 1])).then_inc(bcast_in, 16)
            act.dma_start(oscale[:, :], out_scale.to_broadcast([P, 1])).then_inc(bcast_in, 16)
            act.dma_start(xs[:, TL:, :], dram_rows(x, 1, NCH - 1)).then_inc(xrest_in, 16)

            def relu(j, n):
                T = UNITS * j + n
                act.wait_ge(up_ready, T + 1)
                if T >= NHF:
                    act.wait_ge(lo_done, T - NHF + 1)
                act.activation(hF[:, T % NHF, :], up_ps[n % NU][:, :], ACT.Relu,
                               bias=pcol[:, ROW_B1 + n:ROW_B1 + n + 1]).then_inc(relu_done, 1)

            def hi(j, n):
                T = UNITS * j + n
                if T >= NHS:
                    act.wait_ge(down_ready, T - NHS + 1)
                act.wait_ge(relu_done, T + 1)
                act.copy(hhi[:, T % NHS, :], hF[:, T % NHF, :]).then_inc(hi_act_done, 1)

            def split_w_hi(e):
                act.wait_ge(w1_in[e], 16)
                act.copy(w1hi[:, e, :], w1raw[:, e % NWR, :]).then_inc(whi_done, 1)
                act.wait_ge(w2_in[e], 16)
                act.copy(w2hi[:, e, :], w2raw[:, e % NWR, :]).then_inc(whi_done, 1)

            def p_uT(k):
                act.wait_ge(uT_ready, k + 1)
                if k >= 1:
                    act.wait_ge(z_done, k)
                act.copy(uT[:, :], p_ps[0][:, :]).then_inc(uT_done, 1)

            def p_q(k):
                act.wait_ge(q_ready, k + 1)
                act.activation(qT[:, :], p_ps[1][:, :], ACT.Identity, bias=pcol[:, ROW_BQ:ROW_BQ + 1]
                               ).then_inc(q_done, 1)

            def p_k(k):
                act.wait_ge(k_ready, k + 1)
                act.activation(kT[:, :], p_ps[0][:, :], ACT.Identity, bias=pcol[:, ROW_BK:ROW_BK + 1]
                               ).then_inc(k_done, 1)

            def p_exp(k, b):
                act.wait_ge(nmx_done, NB * k + b + 1)
                if k >= 1:
                    act.wait_ge(attn_done, NB * (k - 1) + b + 1)
                for i in range(2):
                    last = act.activation(ex[:, b, i, :], p_ps[1 - b][:, i * SEQ:(i + 1) * SEQ], ACT.Exp,
                                          bias=nmx[:, b, i:i + 1], scale=SCALE, accum_out=esum[:, b, i:i + 1])
                last.then_inc(exp_done, 1)

            def p_attnT(k, b):
                act.wait_ge(at_ready, NB * k + b + 1)
                act.copy(attnT[:, b, :, :].rearrange("p a s -> p (a s)"), p_ps[1 - b][:, :]).then_inc(at_done, 1)

            def p_context(k):
                act.wait_ge(c_ready, k + 1)
                act.copy(cT[:, :], p_ps[1][:, :]).then_inc(c_done, 1)

            def p_gate_exp(k):
                act.wait_ge(lsh_done, k + 1)
                act.activation(lex[:, :, :], lsh[:, :, :], ACT.Exp).then_inc(lex_done, 1)

            def p_gatesT(k):
                act.wait_ge(gT_ready, k + 1)
                if k >= 1:
                    act.wait_ge(gates_out, 16 * k)
                act.copy(gT[:, :], p_ps[0][0:NE, :]).then_inc(gT_done, 1)

            def r_qk(c):
                act.wait_ge(vT_ready, c + 1)
                act.activation(rqT[:, :], r_ps[1][:, :], ACT.Copy, scale=pcol[:, ROW_QS:ROW_QS + 1])
                act.activation(rkT[:, :], r_ps[1][:, :], ACT.Copy, scale=pcol[:, ROW_KS:ROW_KS + 1]
                               ).then_inc(rqk_done, 1)

            p_uT(0)
            act.wait_ge(pcolT_ready, 1)
            act.copy(pcol[:, :], up_ps[0][:, 0:NROWS]).then_inc(pcol_done, 1)
            act.wait_ge(wvT_ready, 1)
            act.copy(wvT[:, :], up_ps[1][:, 0:P]).then_inc(wvT_done, 1)
            act.wait_ge(pcol_done, 1)
            p_q(0)
            p_k(0)
            act.wait_ge(wvo_ready, 1)
            act.copy(wvo[:, :], down_ps[0][:, 0:P]).then_inc(wvo_done, 1)
            for b in range(NB):
                p_exp(0, b)
            for b in range(NB):
                p_attnT(0, b)
            split_w_hi(0)
            p_context(0)
            split_w_hi(1)
            p_gate_exp(0)
            p_gatesT(0)

            for j in range(PHASES):
                for n in range(UNITS):
                    relu(j, n)
                    if HI_ON_ACT[n]:
                        hi(j, n)
                    if j == 0:
                        if n % 3 == 1 and n // 3 + 2 < NE:
                            split_w_hi(n // 3 + 2)
                        if n == 24:
                            act.wait_ge(dcy_vec, 2)
                            act.activation(dcy[:, 3:4], dcy[:, 2:3], ACT.Exp, scale=-1.0).then_inc(dcy_act, 1)
                            act.wait_ge(dcy_act, 1)
                            act.activation(dcy[:, 4:5], dcy[:, 3:4], ACT.Ln, bias=1.0).then_inc(dcy_act, 1)
                        if n == 27:
                            act.wait_ge(dcy_vec, 4)
                            act.activation(dmask[:, :], expo, ACT.Exp, scale=dcy[:, 6:7]).then_inc(dcy_act, 1)
                    if 1 <= j <= NCH and n == AT_VT:
                        r_qk(j - 1)
                    k = j + 1
                    if k < PHASES:
                        if n == AT_UT:
                            p_uT(k)
                        if n == AT_Q:
                            p_q(k)
                        if n == AT_K:
                            p_k(k)
                        if n in AT_SC:
                            p_exp(k, AT_SC.index(n))
                        if n in AT_AT:
                            p_attnT(k, AT_AT.index(n))
                        if n == AT_C:
                            p_context(k)
                        if n == AT_LG:
                            p_gate_exp(k)
                        if n == AT_GT:
                            p_gatesT(k)

        @block.vector
        def _(dve):
            def hi(j, n):
                T = UNITS * j + n
                if T >= NHS:
                    dve.wait_ge(down_ready, T - NHS + 1)
                dve.wait_ge(relu_done, T + 1)
                dve.tensor_copy(hhi[:, T % NHS, :], hF[:, T % NHF, :]).then_inc(hi_vec_done, 1)

            def lo(j, n):
                T = UNITS * j + n
                if T >= NHS:
                    dve.wait_ge(down_ready, T - NHS + 1)
                dve.wait_ge(hi_act_done if HI_ON_ACT[n] else hi_vec_done, hi_count(j, n, HI_ON_ACT[n]))
                dve.tensor_tensor(hlo[:, T % NHS, :], hF[:, T % NHF, :], hhi[:, T % NHS, :].bitcast(F32),
                                  ALU.subtract).then_inc(lo_done, 1)

            def gate(j, e):
                G = NE * j + e
                dve.wait_ge(down_ready, UNITS * j + DQ * (e + 1))
                if e == 0:
                    dve.wait_ge(gbc_in[j % 2], 16 * (j // 2 + 1))
                if G >= 2:
                    dve.wait_ge(sum_done, G - 1)
                dve.scalar_tensor_tensor(out=gated[:, e % 2, :], in0=down_ps[e % 2][:, :],
                                         scalar=pcol[:, ROW_B2 + e:ROW_B2 + e + 1],
                                         in1=gbc[:, j % 2, e, :], op0=ALU.add, op1=ALU.mult).then_inc(gate_done, 1)

            def norm_stats(chunk, count, st, mv, rs, stat, var, eps):
                for t in range(TL):
                    last = dve.bn_stats(st[:, t, :], row_tile(chunk, t))
                last.then_inc(stat, 1)
                dve.wait_ge(stat, count)
                for t in range(TL):
                    last = dve.bn_aggr(mv[:, t, :], st[:, t, :])
                last.then_inc(var, 1)
                dve.wait_ge(var, count)
                dve.tensor_scalar(rs[:, 0, :], mv[:, :, 1], EPS, None, ALU.add).then_inc(eps, 1)

            def norm_apply(chunk, count, dst, mv, rs, rstd, done):
                dve.wait_ge(rstd, count)
                for t in range(TL):
                    last = dve.tensor_scalar(dst[:, t, :], row_tile(chunk, t), mv[:, t, 0:1], rs[:, 1, t:t + 1],
                                             ALU.subtract, ALU.mult)
                last.then_inc(done, 1)

            def p_norm_stats(k):
                c = k % NCH
                if k == 1:
                    dve.wait_ge(xrest_in, 16)
                if k >= NCH:
                    dve.wait_ge(rx_done, c + 1)
                norm_stats(c, k + 1, st_p, mv_p, rs_p, p_stat, p_var, p_eps)

            def p_norm(k):
                if k >= 1:
                    dve.wait_ge(c_ready, k)
                norm_apply(k % NCH, k + 1, u, mv_p, rs_p, p_rstd, p_u)

            def p_max(k, b):
                dve.wait_ge(sc_ready, NB * k + b + 1)
                dve.tensor_reduce(smx[:, b, :], p_ps[1 - b][:, :].rearrange("p (i s) -> p i s", i=2),
                                  AX_X, ALU.max).then_inc(smx_done, 1)
                dve.wait_ge(smx_done, NB * k + b + 1)
                dve.tensor_scalar(nmx[:, b, :], smx[:, b, :], -SCALE, None, ALU.mult).then_inc(nmx_done, 1)

            def p_attn(k, b):
                dve.wait_ge(exp_done, NB * k + b + 1)
                dve.reciprocal(rsum[:, b, :], esum[:, b, :]).then_inc(rsum_done, 1)
                dve.wait_ge(rsum_done, NB * k + b + 1)
                for i in range(2):
                    last = dve.tensor_scalar(attn[:, b, i, :], ex[:, b, i, :], rsum[:, b, i:i + 1], None, ALU.mult)
                last.then_inc(attn_done, 1)

            def p_z(k):
                par = k % 2
                dve.wait_ge(a_ready, k + 1)
                if k == 0:
                    dve.wait_ge(bvo_done, 1)
                dve.scalar_tensor_tensor(out=facc[:, par, :], in0=p_ps[0][:, :], scalar=bvo[:, 0:1],
                                         in1=uT[:, :], op0=ALU.add, op1=ALU.add).then_inc(z_done, 1)
                dve.wait_ge(z_done, k + 1)
                dve.tensor_copy(zhi[:, par, :], facc[:, par, :]).then_inc(zhi_done, 1)

            def p_zlo(k):
                par = k % 2
                dve.wait_ge(zhi_done, k + 1)
                dve.tensor_tensor(zlo[:, par, :], facc[:, par, :], zhi[:, par, :].bitcast(F32),
                                  ALU.subtract).then_inc(zlo_done, 1)

            def p_gate_shift(k):
                dve.wait_ge(lg_ready, k + 1)
                if k == 0:
                    dve.wait_ge(bcast_in, 48)
                dve.tensor_tensor(lg[:, :, :], p_ps[1][:, 0:TL * NE].rearrange("p (t e) -> p t e", t=TL),
                                  bg_all[:, :].unsqueeze(1).to_broadcast([P, TL, NE]), ALU.add).then_inc(lg_done, 1)
                dve.wait_ge(lg_done, k + 1)
                dve.tensor_reduce(lmx[:, :], lg[:, :, :], AX_X, ALU.max).then_inc(lmx_done, 1)
                dve.wait_ge(lmx_done, k + 1)
                dve.tensor_tensor(lsh[:, :, :], lg[:, :, :], lmx[:, :].unsqueeze(2).to_broadcast([P, TL, NE]),
                                  ALU.subtract).then_inc(lsh_done, 1)

            def p_gate_norm(k):
                dve.wait_ge(lex_done, k + 1)
                dve.tensor_reduce(lsm[:, :], lex[:, :, :], AX_X, ALU.add).then_inc(lsm_done, 1)
                dve.wait_ge(lsm_done, k + 1)
                dve.reciprocal(lrc[:, :], lsm[:, :]).then_inc(lrc_done, 1)
                dve.wait_ge(lrc_done, k + 1)
                dve.tensor_tensor(gts[:, :, :], lex[:, :, :], lrc[:, :].unsqueeze(2).to_broadcast([P, TL, NE]),
                                  ALU.mult).then_inc(gts_done, 1)

            def fold(j):
                dve.wait_ge(fold_ready, j + 1)
                rows = rows_of(j % NCH)
                dve.scalar_tensor_tensor(out=rows, in0=r_ps[0][:, :].rearrange("p (t h) -> p t h", t=TL),
                                         scalar=0.5, in1=rows, op0=ALU.mult, op1=ALU.add).then_inc(fold_done, 1)

            def r_norm_stats(c):
                dve.wait_ge(fold_done, c + 1)
                norm_stats(c, c + 1, st_r, mv_r, rs_r, r_stat, r_var, r_eps)

            def r_norm(c):
                norm_apply(c, c + 1, v, mv_r, rs_r, r_rstd, r_v)

            def r_decay(c, b):
                dve.wait_ge(rsc_ready, NB * c + b + 1)
                dve.wait_ge(dmask_done, 1)
                dve.tensor_tensor(pT[:, b, :], r_ps[b][:, 0:384], dmask[:, :], ALU.mult).then_inc(pT_done, 1)

            def r_add(c):
                dve.wait_ge(r_ready, c + 1)
                rows = rows_of(c)
                dve.scalar_tensor_tensor(out=rows, in0=r_ps[0][:, :].rearrange("p (t h) -> p t h", t=TL),
                                         scalar=oscale[:, 0:1], in1=rows, op0=ALU.mult, op1=ALU.add
                                         ).then_inc(rx_done, 1)

            dve.wait_ge(x0_in, 16)
            p_norm_stats(0)
            p_norm(0)
            dve.wait_ge(bvo_ready, 1)
            dve.wait_ge(pcol_done, 1)
            dve.tensor_tensor(bvo[:, :], down_ps[1][:, 0:1], pcol[:, ROW_BO:ROW_BO + 1], ALU.add).then_inc(bvo_done, 1)
            for b in range(NB):
                p_max(0, b)
            for b in range(NB):
                p_attn(0, b)
            p_z(0)
            p_zlo(0)
            p_gate_shift(0)
            p_gate_norm(0)
            dve.wait_ge(bcast_in, 48)
            dve.tensor_scalar(dcy[:, 1:2], dcy[:, 0:1], -1.0, None, ALU.mult).then_inc(dcy_vec, 1)
            dve.wait_ge(dcy_vec, 1)
            dve.tensor_tensor(dcy[:, 2:3], dcy[:, 0:1], dcy[:, 1:2], ALU.max).then_inc(dcy_vec, 1)
            dve.tensor_scalar(dcy[:, 5:6], dcy[:, 0:1], 0.0, None, ALU.min).then_inc(dcy_vec, 1)

            for j in range(PHASES):
                k = j + 1
                for n in range(UNITS):
                    if j >= 1:
                        if n == AT_FOLD:
                            fold(j - 1)
                        if j <= NCH:
                            if n == AT_RNORM:
                                r_norm_stats(j - 1)
                            if n == AT_RNORM + 2:
                                r_norm(j - 1)
                            if n in AT_RSC:
                                r_decay(j - 1, AT_RSC.index(n))
                            if n == AT_R:
                                r_add(j - 1)
                    if k < PHASES:
                        if n == AT_NORM:
                            p_norm_stats(k)
                        if n == AT_NORM + 2:
                            p_norm(k)
                        if n in AT_SC:
                            p_max(k, AT_SC.index(n))
                        if n - 1 in AT_SC:
                            p_attn(k, AT_SC.index(n - 1))
                        if n == AT_A:
                            p_z(k)
                        if n == AT_A + 1:
                            p_zlo(k)
                        if n == AT_LG:
                            p_gate_shift(k)
                        if n == AT_LG + 1:
                            p_gate_norm(k)
                    if j == 0 and n == 26:
                        dve.wait_ge(dcy_act, 2)
                        dve.wait_ge(dcy_vec, 3)
                        dve.tensor_tensor(dcy[:, 6:7], dcy[:, 5:6], dcy[:, 4:5], ALU.subtract).then_inc(dcy_vec, 1)
                    if j == 0 and n == 29:
                        dve.wait_ge(dcy_act, 3)
                        dve.tensor_tensor(dmask[:, :], dmask[:, :], causal, ALU.mult).then_inc(dmask_done, 1)
                    if not HI_ON_ACT[n]:
                        hi(j, n)
                    lo(j, n)
                    m = n - LAG - 1
                    if m >= 0 and m % DQ == DQ - 1:
                        gate(j, m // DQ)
                    elif m < 0 and (m + UNITS) % DQ == DQ - 1 and j >= 1:
                        gate(j - 1, NE - 1)
            gate(PHASES - 1, NE - 1)
            fold(PHASES - 1)

        @block.gpsimd
        def _(pool):
            def rstd(count, rs, eps, done):
                pool.wait_ge(eps, count)
                pool.tensor_tensor(rs[:, 1, :], rs[:, 0, :], mhalf[:, :], ALU.pow).then_inc(done, 1)

            def split_w_lo(e):
                pool.wait_ge(whi_done, 2 * e + 1)
                pool.tensor_tensor(w1lo[:, e, :], w1raw[:, e % NWR, :], w1hi[:, e, :].bitcast(F32), ALU.subtract
                                   ).then_inc(wlo_done, 1)
                pool.wait_ge(whi_done, 2 * e + 2)
                pool.tensor_tensor(w2lo[:, e, :], w2raw[:, e % NWR, :], w2hi[:, e, :].bitcast(F32), ALU.subtract
                                   ).then_inc(wlo_done, 1)

            def add(j, e):
                G = NE * j + e
                pool.wait_ge(gate_done, G + 1)
                if G >= 1:
                    pool.wait_ge(sum_done, G)
                acc = facc[:, j % 2, :]
                pool.tensor_tensor(acc, acc, gated[:, e % 2, :], ALU.add).then_inc(sum_done, 1)

            pool.memset(mhalf[:, :], -0.5).then_inc(mhalf_set, 1)
            pool.wait_ge(mhalf_set, 1)
            rstd(1, rs_p, p_eps, p_rstd)
            split_w_lo(0)
            split_w_lo(1)
            for j in range(PHASES):
                if j + 1 < PHASES:
                    rstd(j + 2, rs_p, p_eps, p_rstd)
                if j >= 1:
                    add(j - 1, NE - 1)
                    if j <= NCH:
                        rstd(j, rs_r, r_eps, r_rstd)
                for e in range(NE - 1):
                    if j == 0 and e + 2 < NE:
                        split_w_lo(e + 2)
                    add(j, e)
            add(PHASES - 1, NE - 1)


SCALE = float(P) ** -0.5


_INS = ["L0_attn_x", "L0_attn_decay_logit", "L0_attn_out_scale", "L0_attn_q_scale", "L0_attn_k_scale",
        "L0_ffn_Wq", "L0_ffn_bq", "L0_ffn_Wk", "L0_ffn_bk", "L0_ffn_Wv", "L0_ffn_bv", "L0_ffn_Wo",
        "L0_ffn_bo", "L0_ffn_Wg", "L0_ffn_bg", "L0_ffn_W1", "L0_ffn_b1", "L0_ffn_W2", "L0_ffn_b2"]


def kernel(**inputs):
    import numpy as np
    import concourse.bacc as bacc
    from concourse.bass_utils import run_bass_kernel_spmd as run

    nc = bacc.Bacc("TRN2", target_bir_lowering=False, num_devices=1)
    arrays, args = {}, []
    for name in _INS:
        a = np.ascontiguousarray(inputs[name])
        if a.ndim == 0:
            a = a.reshape(1, 1)
        arrays[f"in_{name}"] = a
        args.append(nc.dram_tensor(f"in_{name}", a.shape, mybir.dt.from_np(a.dtype), kind="ExternalInput").ap())

    s = np.arange(P)[:, None]
    diff = np.concatenate([s - np.arange(P)[None, :], s + P - np.arange(SEQ)[None, :]], axis=1)
    shapes = np.concatenate([np.eye(P), np.maximum(diff - 1, 0), diff > 0], axis=1).astype(np.float32)
    arrays["shapes"] = shapes
    args.append(nc.dram_tensor("shapes", shapes.shape, F32, kind="ExternalInput").ap())
    args.append(nc.dram_tensor("gates_scratch", (2, NE, CH), F32, kind="Internal").ap())
    x = inputs["L0_attn_x"]
    args.append(nc.dram_tensor("out_0", tuple(x.shape), F32, kind="ExternalOutput").ap())
    macaron(nc, *args)
    r = run(nc, [arrays], core_ids=[0])
    return r.results[0]["out_0"]
```

```python
from contextlib import ExitStack

import concourse.bass as bass
from concourse import mybir

F32 = mybir.dt.float32
F32R = mybir.dt.float32r
ALU = mybir.AluOpType
ACT = mybir.ActivationFunctionType
AX_X = mybir.AxisListType.X

P = 128
NCH = 4
CH = 512
TL = CH // P
SEQ = 256
NB = CH // SEQ
NE = 8
DQ = 4
UNITS = NE * DQ
PHASES = 2 * NCH
EPS = 1e-5

LAG = 3
NU = 3
WARM = 10
NWR = 4
NHF = 3
NHS = 4

COL_B1, COL_B2 = 0, 32
COL_BQ, COL_BK, COL_BV, COL_BO, COL_QS, COL_KS, COL_DECAY, COL_OSCALE = range(40, 48)
COL_BG = 48
NCOLS = COL_BG + NE
NATTN = 4 * P + NE

AT_NORM = 0
AT_UT, AT_Q, AT_K = 4, 6, 6
AT_SC = (9, 11)
AT_AT = (13, 15)
AT_C, AT_A, AT_LG, AT_GT = 17, 22, 25, 30
AT_FOLD = 9
AT_RNORM = 10
AT_VT = 14
AT_RSC = (17, 19)
AT_R = 22

PHASE0_LATER = 0


def side_unit(j, n):
    if j > 0 or n < AT_UT:
        return n
    return n - PHASE0_LATER if n >= AT_UT + PHASE0_LATER else -1


HI_ON_ACT = [n not in (2, 14, 25, 27, 31) for n in range(UNITS)]


def macaron(nc, x, experts, attn_weights, params, identity, decay_shapes, gates_dram, out):
    ctx = ExitStack()
    with ctx:
        def sb(name, shape, dt=F32):
            return ctx.enter_context(nc.sbuf_tensor(name, shape, dt))

        def bank(name):
            return ctx.enter_context(nc.psum_tensor(name, [P, 512], F32))

        def sem(name):
            return ctx.enter_context(nc.semaphore(name))

        xs = sb("xs", [P, NCH * TL, P])
        wraw = sb("wraw", [P, NWR, 2, CH])
        v = wraw[:, 0, 0, :].rearrange("p (t h) -> p t h", t=TL)
        rqT = wraw[:, 0, 1, :]
        rkT = wraw[:, 1, 0, :]
        pT = wraw[:, 2, :, 0:384]
        w1hi = sb("w1hi", [P, NE, CH], F32R)
        w1lo = sb("w1lo", [P, NE, CH], F32R)
        w2hi = sb("w2hi", [P, NE, CH], F32R)
        w2lo = sb("w2lo", [P, NE, CH], F32R)
        wattn = sb("wattn", [P, NATTN])
        wvT, wo = (wattn[:, i * P:(i + 1) * P] for i in (2, 3))
        wg = wattn[:, 4 * P:NATTN]
        wqk_hi = sb("wqk_hi", [P, 2, P], F32R)
        wqk_lo = sb("wqk_lo", [P, 2, P], F32R)
        wvo = sb("wvo", [P, P])
        wvo_hi = sb("wvo_hi", [P, P], F32R)
        wvo_lo = sb("wvo_lo", [P, P], F32R)
        bvo = sb("bvo", [P, 1])
        pcol = sb("pcol", [P, NCOLS])
        ident_t = sb("ident_t", [P, P])
        ident = ident_t[:, :]
        shp = sb("shp", [P, 2, 384])
        dcy = sb("dcy", [P, 8])
        dmask = shp[:, 1, :]
        mhalf = sb("mhalf", [P, TL])
        u = sb("u", [P, TL, P])
        st_p = sb("st_p", [P, TL, 6])
        mv_p = sb("mv_p", [P, TL, 2])
        rs_p = sb("rs_p", [P, 2, TL])
        st_r = sb("st_r", [P, TL, 6])
        mv_r = sb("mv_r", [P, TL, 2])
        rs_r = sb("rs_r", [P, 2, TL])
        uT = sb("uT", [P, CH])
        u_hi = sb("u_hi", [P, TL, P], F32R)
        u_lo = sb("u_lo", [P, TL, P], F32R)
        uT_hi = sb("uT_hi", [P, CH], F32R)
        uT_lo = sb("uT_lo", [P, CH], F32R)
        qT_hi = sb("qT_hi", [P, CH], F32R)
        qT_lo = sb("qT_lo", [P, CH], F32R)
        kT_hi = sb("kT_hi", [P, CH], F32R)
        kT_lo = sb("kT_lo", [P, CH], F32R)
        smx = sb("smx", [P, NB, 2])
        nmx = sb("nmx", [P, NB, 2])
        esum = sb("esum", [P, NB, 2])
        rsum = sb("rsum", [P, NB, 2])
        ex = sb("ex", [P, NB, 2, SEQ])
        attn = ex
        attnT_hi = sb("attnT_hi", [P, NB, 2, SEQ], F32R)
        attnT_lo = sb("attnT_lo", [P, NB, 2, SEQ], F32R)
        cT_hi = sb("cT_hi", [P, CH], F32R)
        cT_lo = sb("cT_lo", [P, CH], F32R)
        facc = sb("facc", [P, 2, CH])
        zhi = sb("zhi", [P, 2, CH], F32R)
        zlo = sb("zlo", [P, 2, CH], F32R)
        lg = sb("lg", [P, TL, NE])
        lmx = sb("lmx", [P, TL])
        lsh = sb("lsh", [P, TL, NE])
        lex = sb("lex", [P, TL, NE])
        lsm = sb("lsm", [P, TL])
        lrc = sb("lrc", [P, TL])
        gts = sb("gts", [P, TL, NE])
        gT = sb("gT", [NE, CH])
        gbc = sb("gbc", [P, 2, NE, CH])
        hF = sb("hF", [P, NHF, CH])
        hhi = sb("hhi", [P, NHS, CH], F32R)
        hlo = sb("hlo", [P, NHS, CH], F32R)
        gated = sb("gated", [P, 2, CH])

        up_ps = [bank(f"up_ps{i}") for i in range(NU)]
        down_ps = [bank(f"down_ps{i}") for i in range(2)]
        p_ps = [bank(f"p_ps{i}") for i in range(2)]
        r_ps = bank("r_ps")

        x0_in = sem("x0_in")
        ident_in = sem("ident_in")
        wattn_in = sem("wattn_in")
        params_in = sem("params_in")
        shapes_in = sem("shapes_in")
        xrest_in = sem("xrest_in")
        w_in = [sem(f"w_in{e}") for e in range(NE)]
        mhalf_set = sem("mhalf_set")
        whi_done = sem("whi_done")
        wlo_done = sem("wlo_done")
        wqk_hi_done, wqk_lo_done = sem("wqk_hi_done"), sem("wqk_lo_done")
        wvo_ready, wvo_done = sem("wvo_ready"), sem("wvo_done")
        wvo_hi_done, wvo_lo_done = sem("wvo_hi_done"), sem("wvo_lo_done")
        u_hi_done, u_lo_done = sem("u_hi_done"), sem("u_lo_done")
        bvo_ready, bvo_done = sem("bvo_ready"), sem("bvo_done")
        dcy_vec, dcy_act, dmask_done = sem("dcy_vec"), sem("dcy_act"), sem("dmask_done")
        up_ready, relu_done = sem("up_ready"), sem("relu_done")
        hi_act_done, hi_vec_done, lo_done = sem("hi_act_done"), sem("hi_vec_done"), sem("lo_done")
        down_ready, gate_done, sum_done = sem("down_ready"), sem("gate_done"), sem("sum_done")
        p_stat, p_var, p_eps, p_rstd, p_u = (sem(f"p_{n}") for n in ("stat", "var", "eps", "rstd", "u"))
        r_stat, r_var, r_eps, r_rstd, r_v = (sem(f"r_{n}") for n in ("stat", "var", "eps", "rstd", "v"))
        uT_ready, uT_done = sem("uT_ready"), sem("uT_done")
        uT_hi_done, uT_lo_done = sem("uT_hi_done"), sem("uT_lo_done")
        q_ready, q_hi_done, q_lo_done = sem("q_ready"), sem("q_hi_done"), sem("q_lo_done")
        k_ready, k_hi_done, k_lo_done = sem("k_ready"), sem("k_hi_done"), sem("k_lo_done")
        sc_ready, smx_done, nmx_done = sem("sc_ready"), sem("smx_done"), sem("nmx_done")
        exp_done, rsum_done, attn_done = sem("exp_done"), sem("rsum_done"), sem("attn_done")
        at_ready, at_hi_done, at_lo_done = sem("at_ready"), sem("at_hi_done"), sem("at_lo_done")
        c_ready, c_hi_done, c_lo_done = sem("c_ready"), sem("c_hi_done"), sem("c_lo_done")
        a_ready, z_done, zhi_done, zlo_done = sem("a_ready"), sem("z_done"), sem("zhi_done"), sem("zlo_done")
        lg_ready, lg_done, lmx_done, lsh_done = sem("lg_ready"), sem("lg_done"), sem("lmx_done"), sem("lsh_done")
        lex_done, lsm_done, lrc_done, gts_done = sem("lex_done"), sem("lsm_done"), sem("lrc_done"), sem("gts_done")
        gT_ready, gT_done = sem("gT_ready"), sem("gT_done")
        gates_out = sem("gates_out")
        gbc_in = [sem(f"gbc_in{i}") for i in range(2)]
        fold_ready, fold_done = sem("fold_ready"), sem("fold_done")
        vT_ready, rqk_done = sem("vT_ready"), sem("rqk_done")
        rsc_ready, pT_done = sem("rsc_ready"), sem("pT_done")
        r_ready, rx_done = sem("r_ready"), sem("rx_done")
        stored = sem("stored")

        per_phase = {True: HI_ON_ACT.count(True), False: HI_ON_ACT.count(False)}

        def hi_count(j, n, on_act):
            return per_phase[on_act] * j + HI_ON_ACT[:n + 1].count(on_act)

        def rows_of(chunk):
            return xs[:, bass.ds(chunk * TL, TL), :] if not isinstance(chunk, int) else \
                xs[:, chunk * TL:(chunk + 1) * TL, :]

        def row_tile(chunk, t):
            return xs[:, bass.ds(chunk * TL + t, 1), :] if not isinstance(chunk, int) else \
                xs[:, chunk * TL + t, :]

        block = ctx.enter_context(nc.Block())

        @block.sync
        def _(sp):
            sp.dma_start(rows_of(0), x[:, 0:TL, :]).then_inc(x0_in, 16)
            sp.dma_start(ident, identity).then_inc(ident_in, 16)
            sp.dma_start(pcol[:, :], params).then_inc(params_in, 16)

            def load_expert(e):
                if e >= NWR:
                    sp.wait_ge(wlo_done, 2 * (e - NWR) + 2)
                sp.dma_start(wraw[:, e % NWR, :, :], experts[:, e, :, :]).then_inc(w_in[e], 16)

            def spread_gates(k):
                par = k % 2
                sp.wait_ge(gT_done, k + 1)
                if k >= 2:
                    sp.wait_ge(gbc_in[par], 16 * (k // 2))
                sp.dma_start(gates_dram[par], gT[:, :]).then_inc(gates_out, 16)
                sp.wait_ge(gates_out, 16 * (k + 1))
                if k >= 2:
                    sp.wait_ge(gate_done, NE * (k - 1))
                sp.dma_start(gbc[:, par, :, :], gates_dram[par:par + 1].to_broadcast([P, NE, CH])
                             ).then_inc(gbc_in[par], 16)

            def store(j):
                c = j % NCH
                sp.wait_ge(fold_done, j + 1)
                sp.dma_start(out[:, c * TL:(c + 1) * TL, :], rows_of(c)).then_inc(stored, 16)

            for e in range(NWR):
                load_expert(e)
            sp.dma_start(xs[:, TL:, :], x[:, TL:, :]).then_inc(xrest_in, 16)
            sp.dma_start(shp[:, :, :], decay_shapes).then_inc(shapes_in, 16)
            spread_gates(0)
            for e in range(NWR, NE):
                load_expert(e)
            for j in range(PHASES):
                if j > NCH:
                    store(j - 1)
                if j + 1 < PHASES:
                    spread_gates(j + 1)
            store(PHASES - 1)
            sp.wait_ge(stored, 16 * NCH)

        @block.tensor
        def _(pe):
            def up(j, n):
                e, d = divmod(n, DQ)
                T = UNITS * j + n
                if n == 0:
                    pe.wait_ge(zhi_done, j + 1)
                if j == 0 and d == 0:
                    pe.wait_ge(wlo_done, 2 * e + 1)
                if T >= NU:
                    pe.wait_ge(relu_done, T - NU + 1)
                dst = up_ps[T % NU][:, :]
                cols = slice(P * d, P * d + P)
                pe.matmul(dst, w1lo[:, e, cols], zhi[:, j % 2, :], start=True, stop=False)
                pe.matmul(dst, w1hi[:, e, cols], zhi[:, j % 2, :], start=False, stop=False)
                if n == 0:
                    pe.wait_ge(zlo_done, j + 1)
                pe.matmul(dst, w1hi[:, e, cols], zlo[:, j % 2, :], start=False, stop=True).then_inc(up_ready, 1)

            def down(j, n):
                e, d = divmod(n, DQ)
                T = UNITS * j + n
                if j == 0 and d == 0:
                    pe.wait_ge(wlo_done, 2 * e + 2)
                G = NE * j + e
                if d == 0 and G >= 2:
                    pe.wait_ge(gate_done, G - 1)
                pe.wait_ge(hi_act_done if HI_ON_ACT[n] else hi_vec_done, hi_count(j, n, HI_ON_ACT[n]))
                dst = down_ps[e % 2][:, :]
                cols = slice(P * d, P * d + P)
                h = T % NHS
                pe.matmul(dst, w2lo[:, e, cols], hhi[:, h, :], start=(d == 0), stop=False)
                pe.matmul(dst, w2hi[:, e, cols], hhi[:, h, :], start=False, stop=False)
                pe.wait_ge(lo_done, T + 1)
                pe.matmul(dst, w2hi[:, e, cols], hlo[:, h, :], start=False, stop=(d == DQ - 1)
                          ).then_inc(down_ready, 1)

            def transpose_tiles(dst, src_of, done):
                for t in range(TL):
                    last = pe.transpose(dst[:, t * P:(t + 1) * P], src_of(t), ident)
                last.then_inc(done, 1)

            def p_uT(k):
                pe.wait_ge(p_u, k + 1)
                if k >= 1:
                    pe.wait_ge(gT_done, k)
                transpose_tiles(p_ps[0], lambda t: u[:, t, :], uT_ready)

            def p_q(k):
                pe.wait_ge(uT_hi_done, k + 1)
                dst = p_ps[1][:, :]
                pe.matmul(dst, wqk_lo[:, 0, :], uT_hi[:, :], start=True, stop=False)
                pe.matmul(dst, wqk_hi[:, 0, :], uT_hi[:, :], start=False, stop=False)
                pe.wait_ge(uT_lo_done, k + 1)
                pe.matmul(dst, wqk_hi[:, 0, :], uT_lo[:, :], start=False, stop=True).then_inc(q_ready, 1)

            def p_k(k):
                dst = p_ps[0][:, :]
                pe.matmul(dst, wqk_lo[:, 1, :], uT_hi[:, :], start=True, stop=False)
                pe.matmul(dst, wqk_hi[:, 1, :], uT_hi[:, :], start=False, stop=False)
                pe.matmul(dst, wqk_hi[:, 1, :], uT_lo[:, :], start=False, stop=True).then_inc(k_ready, 1)

            def p_scores(k, b):
                pe.wait_ge(q_lo_done, k + 1)
                pe.wait_ge(k_lo_done, k + 1)
                keys = slice(b * SEQ, (b + 1) * SEQ)
                for i in range(2):
                    dst = p_ps[1 - b][:, i * SEQ:(i + 1) * SEQ]
                    qs = slice(b * SEQ + i * P, b * SEQ + (i + 1) * P)
                    pe.matmul(dst, qT_lo[:, qs], kT_hi[:, keys], start=True, stop=False)
                    pe.matmul(dst, qT_hi[:, qs], kT_hi[:, keys], start=False, stop=False)
                    last = pe.matmul(dst, qT_hi[:, qs], kT_lo[:, keys], start=False, stop=True)
                last.then_inc(sc_ready, 1)

            def p_attnT(k, b):
                pe.wait_ge(attn_done, NB * k + b + 1)
                for kt in range(2):
                    for i in range(2):
                        at = kt * SEQ + i * P
                        last = pe.transpose(p_ps[1 - b][:, at:at + P], attn[:, b, i, kt * P:(kt + 1) * P], ident)
                last.then_inc(at_ready, 1)

            def p_context(k):
                pe.wait_ge(u_lo_done, k + 1)
                for b in range(NB):
                    pe.wait_ge(at_lo_done, NB * k + b + 1)
                    dst = p_ps[1][:, b * SEQ:(b + 1) * SEQ]
                    for kt in range(2):
                        t = 2 * b + kt
                        pe.matmul(dst, u_lo[:, t, :], attnT_hi[:, b, kt, :], start=(kt == 0), stop=False)
                        pe.matmul(dst, u_hi[:, t, :], attnT_hi[:, b, kt, :], start=False, stop=False)
                        last = pe.matmul(dst, u_hi[:, t, :], attnT_lo[:, b, kt, :], start=False, stop=(kt == 1))
                last.then_inc(c_ready, 1)

            def p_project(k):
                if k == 0:
                    pe.wait_ge(wvo_lo_done, 1)
                pe.wait_ge(c_hi_done, k + 1)
                dst = p_ps[0][:, :]
                pe.matmul(dst, wvo_lo[:, :], cT_hi[:, :], start=True, stop=False)
                pe.matmul(dst, wvo_hi[:, :], cT_hi[:, :], start=False, stop=False)
                pe.wait_ge(c_lo_done, k + 1)
                pe.matmul(dst, wvo_hi[:, :], cT_lo[:, :], start=False, stop=True).then_inc(a_ready, 1)

            def p_logits(k):
                pe.wait_ge(z_done, k + 1)
                for t in range(TL):
                    last = pe.matmul(p_ps[1][:, t * NE:(t + 1) * NE], facc[:, k % 2, t * P:(t + 1) * P],
                                     wg, start=True, stop=True)
                last.then_inc(lg_ready, 1)

            def p_gatesT(k):
                pe.wait_ge(gts_done, k + 1)
                for t in range(TL):
                    last = pe.transpose(p_ps[0][0:NE, t * P:(t + 1) * P], gts[:, t, :], ident)
                last.then_inc(gT_ready, 1)

            def fold(j):
                pe.wait_ge(sum_done, NE * (j + 1))
                if 1 <= j <= NCH:
                    pe.wait_ge(rx_done, j)
                elif j > NCH:
                    pe.wait_ge(fold_done, j)
                transpose_tiles(r_ps, lambda t: facc[:, j % 2, t * P:(t + 1) * P], fold_ready)

            def r_vT(c):
                pe.wait_ge(r_v, c + 1)
                transpose_tiles(r_ps, lambda t: v[:, t, :], vT_ready)

            def r_scores(c, b):
                pe.wait_ge(rqk_done, c + 1)
                if b:
                    pe.wait_ge(pT_done, NB * c + b)
                o = b * SEQ
                pe.matmul(r_ps[:, 0:P], rkT[:, o:o + P], rqT[:, o:o + P], start=True, stop=True)
                pe.matmul(r_ps[:, P:P + SEQ], rkT[:, o + P:o + SEQ], rqT[:, o:o + SEQ],
                          start=True, stop=True).then_inc(rsc_ready, 1)

            def r_retrieve(c):
                pe.wait_ge(pT_done, NB * (c + 1))
                for b in range(NB):
                    t0 = r_ps[:, (2 * b) * P:(2 * b + 1) * P]
                    t1 = r_ps[:, (2 * b + 1) * P:(2 * b + 2) * P]
                    pe.matmul(t0, pT[:, b, 0:P], v[:, 2 * b, :], start=True, stop=False)
                    pe.matmul(t0, pT[:, b, P:2 * P], v[:, 2 * b + 1, :], start=False, stop=True)
                    last = pe.matmul(t1, pT[:, b, 2 * P:3 * P], v[:, 2 * b + 1, :], start=True, stop=True)
                last.then_inc(r_ready, 1)

            pe.wait_ge(ident_in, 16)
            for _ in range(WARM):
                pe.matmul(up_ps[0][:, 0:P], ident, ident, start=True, stop=True)
            p_uT(0)
            pe.wait_ge(wattn_in, 16)
            pe.wait_ge(wqk_lo_done, 1)
            p_q(0)
            p_k(0)
            pe.matmul(down_ps[0][:, 0:P], wvT, wo, start=True, stop=True).then_inc(wvo_ready, 1)
            pe.wait_ge(params_in, 16)
            pe.matmul(down_ps[1][:, 0:1], wo, pcol[:, COL_BV:COL_BV + 1], start=True, stop=True
                      ).then_inc(bvo_ready, 1)
            for b in range(NB):
                p_scores(0, b)
            for b in range(NB):
                p_attnT(0, b)
            p_context(0)
            p_project(0)
            pe.wait_ge(bvo_done, 1)

            for j in range(PHASES):
                for n in range(UNITS):
                    up(j, n)
                    if n >= LAG:
                        down(j, n - LAG)
                    elif j >= 1:
                        down(j - 1, UNITS + n - LAG)
                    if j == 0 and n == 0:
                        p_logits(0)
                    if j == 0 and n == 2:
                        p_gatesT(0)
                    if j >= 1:
                        if n == AT_FOLD:
                            fold(j - 1)
                        if j <= NCH:
                            if n == AT_VT:
                                r_vT(j - 1)
                            if n in AT_RSC:
                                r_scores(j - 1, AT_RSC.index(n))
                            if n == AT_R:
                                r_retrieve(j - 1)
                    k, at = j + 1, side_unit(j, n)
                    if k < PHASES:
                        if at == AT_UT:
                            p_uT(k)
                        if at == AT_Q:
                            p_q(k)
                        if at == AT_K:
                            p_k(k)
                        if at in AT_SC:
                            p_scores(k, AT_SC.index(at))
                        if at in AT_AT:
                            p_attnT(k, AT_AT.index(at))
                        if at == AT_C:
                            p_context(k)
                        if at == AT_A:
                            p_project(k)
                        if at == AT_LG:
                            p_logits(k)
                        if at == AT_GT:
                            p_gatesT(k)
            for n in range(UNITS - LAG, UNITS):
                down(PHASES - 1, n)
            fold(PHASES - 1)

        @block.scalar
        def _(act):
            act.dma_start(wattn[:, :], attn_weights).then_inc(wattn_in, 16)

            def relu(j, n):
                T = UNITS * j + n
                act.wait_ge(up_ready, T + 1)
                if T >= NHF:
                    act.wait_ge(lo_done, T - NHF + 1)
                act.activation(hF[:, T % NHF, :], up_ps[T % NU][:, :], ACT.Relu,
                               bias=pcol[:, COL_B1 + n:COL_B1 + n + 1]).then_inc(relu_done, 1)

            def hi(j, n):
                T = UNITS * j + n
                act.wait_ge(up_ready, T + 1)
                if T >= NHS:
                    act.wait_ge(down_ready, T - NHS + 1)
                act.activation(hhi[:, T % NHS, :], up_ps[T % NU][:, :], ACT.Relu,
                               bias=pcol[:, COL_B1 + n:COL_B1 + n + 1]).then_inc(hi_act_done, 1)

            def split_w_hi(e):
                act.wait_ge(w_in[e], 16)
                act.copy(w1hi[:, e, :], wraw[:, e % NWR, 0, :]).then_inc(whi_done, 1)
                act.copy(w2hi[:, e, :], wraw[:, e % NWR, 1, :]).then_inc(whi_done, 1)

            def p_uT(k):
                act.wait_ge(uT_ready, k + 1)
                if k >= 1:
                    act.wait_ge(z_done, k)
                act.copy(uT[:, :], p_ps[0][:, :]).then_inc(uT_done, 1)

            def p_u_hi(k):
                act.wait_ge(p_u, k + 1)
                if k >= 1:
                    act.wait_ge(c_ready, k)
                act.copy(u_hi[:, :, :], u[:, :, :]).then_inc(u_hi_done, 1)

            def p_q(k):
                act.wait_ge(q_ready, k + 1)
                act.activation(qT_hi[:, :], p_ps[1][:, :], ACT.Identity, bias=pcol[:, COL_BQ:COL_BQ + 1]
                               ).then_inc(q_hi_done, 1)

            def p_k(k):
                act.wait_ge(k_ready, k + 1)
                act.activation(kT_hi[:, :], p_ps[0][:, :], ACT.Identity, bias=pcol[:, COL_BK:COL_BK + 1]
                               ).then_inc(k_hi_done, 1)

            def p_exp(k, b):
                act.wait_ge(nmx_done, NB * k + b + 1)
                if k >= 1:
                    act.wait_ge(attn_done, NB * (k - 1) + b + 1)
                for i in range(2):
                    last = act.activation(ex[:, b, i, :], p_ps[1 - b][:, i * SEQ:(i + 1) * SEQ], ACT.Exp,
                                          bias=nmx[:, b, i:i + 1], scale=SCALE, accum_out=esum[:, b, i:i + 1])
                last.then_inc(exp_done, 1)

            def p_attnT(k, b):
                act.wait_ge(at_ready, NB * k + b + 1)
                act.copy(attnT_hi[:, b, :, :].rearrange("p a s -> p (a s)"), p_ps[1 - b][:, :]).then_inc(at_hi_done, 1)

            def p_context(k):
                act.wait_ge(c_ready, k + 1)
                act.copy(cT_hi[:, :], p_ps[1][:, :]).then_inc(c_hi_done, 1)

            def p_gate_exp(k):
                act.wait_ge(lsh_done, k + 1)
                act.activation(lex[:, :, :], lsh[:, :, :], ACT.Exp).then_inc(lex_done, 1)

            def p_gatesT(k):
                act.wait_ge(gT_ready, k + 1)
                if k >= 1:
                    act.wait_ge(gates_out, 16 * k)
                act.copy(gT[:, :], p_ps[0][0:NE, :]).then_inc(gT_done, 1)

            def r_qk(c):
                act.wait_ge(vT_ready, c + 1)
                act.activation(rqT, r_ps[:, :], ACT.Copy, scale=pcol[:, COL_QS:COL_QS + 1])
                act.activation(rkT, r_ps[:, :], ACT.Copy, scale=pcol[:, COL_KS:COL_KS + 1]
                               ).then_inc(rqk_done, 1)

            act.wait_ge(wattn_in, 16)
            act.copy(wqk_hi[:, :, :].rearrange("p a h -> p (a h)"), wattn[:, 0:2 * P]).then_inc(wqk_hi_done, 1)
            p_uT(0)
            p_u_hi(0)
            act.wait_ge(params_in, 16)
            p_q(0)
            p_k(0)
            act.wait_ge(wvo_ready, 1)
            act.copy(wvo[:, :], down_ps[0][:, 0:P]).then_inc(wvo_done, 1)
            act.wait_ge(wvo_done, 1)
            act.copy(wvo_hi[:, :], wvo[:, :]).then_inc(wvo_hi_done, 1)
            for b in range(NB):
                p_exp(0, b)
            for b in range(NB):
                p_attnT(0, b)
            split_w_hi(0)
            p_context(0)
            split_w_hi(1)

            for j in range(PHASES):
                for n in range(UNITS):
                    if HI_ON_ACT[n]:
                        hi(j, n)
                    relu(j, n)
                    if j == 0 and n == 0:
                        p_gate_exp(0)
                    if j == 0 and n == 2:
                        p_gatesT(0)
                    if j == 0:
                        if n % 3 == 1 and n // 3 + 2 < NE:
                            split_w_hi(n // 3 + 2)
                        if n == 24:
                            act.wait_ge(dcy_vec, 2)
                            act.activation(dcy[:, 3:4], dcy[:, 2:3], ACT.Exp, scale=-1.0).then_inc(dcy_act, 1)
                            act.wait_ge(dcy_act, 1)
                            act.activation(dcy[:, 4:5], dcy[:, 3:4], ACT.Ln, bias=1.0).then_inc(dcy_act, 1)
                        if n == 27:
                            act.wait_ge(dcy_vec, 4)
                            act.wait_ge(shapes_in, 16)
                            act.activation(dmask, dmask, ACT.Exp, scale=dcy[:, 6:7]).then_inc(dcy_act, 1)
                    if 1 <= j <= NCH and n == AT_VT:
                        r_qk(j - 1)
                    k, at = j + 1, side_unit(j, n)
                    if k < PHASES:
                        if at == AT_UT:
                            p_uT(k)
                        if at == AT_UT + 1:
                            p_u_hi(k)
                        if at == AT_Q:
                            p_q(k)
                        if at == AT_K:
                            p_k(k)
                        if at in AT_SC:
                            p_exp(k, AT_SC.index(at))
                        if at in AT_AT:
                            p_attnT(k, AT_AT.index(at))
                        if at == AT_C:
                            p_context(k)
                        if at == AT_LG:
                            p_gate_exp(k)
                        if at == AT_GT:
                            p_gatesT(k)

        @block.vector
        def _(dve):
            def hi(j, n):
                T = UNITS * j + n
                if T >= NHS:
                    dve.wait_ge(down_ready, T - NHS + 1)
                dve.wait_ge(relu_done, T + 1)
                dve.tensor_copy(hhi[:, T % NHS, :], hF[:, T % NHF, :]).then_inc(hi_vec_done, 1)

            def lo(j, n):
                T = UNITS * j + n
                if T >= NHS:
                    dve.wait_ge(down_ready, T - NHS + 1)
                dve.wait_ge(relu_done, T + 1)
                dve.wait_ge(hi_act_done if HI_ON_ACT[n] else hi_vec_done, hi_count(j, n, HI_ON_ACT[n]))
                dve.tensor_tensor(hlo[:, T % NHS, :], hF[:, T % NHF, :], hhi[:, T % NHS, :].bitcast(F32),
                                  ALU.subtract).then_inc(lo_done, 1)

            def gate(j, e):
                G = NE * j + e
                dve.wait_ge(down_ready, UNITS * j + DQ * (e + 1))
                if e == 0:
                    dve.wait_ge(gbc_in[j % 2], 16 * (j // 2 + 1))
                if G >= 2:
                    dve.wait_ge(sum_done, G - 1)
                dve.scalar_tensor_tensor(out=gated[:, e % 2, :], in0=down_ps[e % 2][:, :],
                                         scalar=pcol[:, COL_B2 + e:COL_B2 + e + 1],
                                         in1=gbc[:, j % 2, e, :], op0=ALU.add, op1=ALU.mult).then_inc(gate_done, 1)

            def norm_stats(chunk, count, st, mv, rs, stat, var, eps):
                for t in range(TL):
                    last = dve.bn_stats(st[:, t, :], row_tile(chunk, t))
                last.then_inc(stat, 1)
                dve.wait_ge(stat, count)
                for t in range(TL):
                    last = dve.bn_aggr(mv[:, t, :], st[:, t, :])
                last.then_inc(var, 1)
                dve.wait_ge(var, count)
                dve.tensor_scalar(rs[:, 0, :], mv[:, :, 1], EPS, None, ALU.add).then_inc(eps, 1)

            def norm_apply(chunk, count, dst, mv, rs, rstd, done):
                dve.wait_ge(rstd, count)
                for t in range(TL):
                    last = dve.tensor_scalar(dst[:, t, :], row_tile(chunk, t), mv[:, t, 0:1], rs[:, 1, t:t + 1],
                                             ALU.subtract, ALU.mult)
                last.then_inc(done, 1)

            def p_norm_stats(k):
                c = k % NCH
                if k == 1:
                    dve.wait_ge(xrest_in, 16)
                if k >= NCH:
                    dve.wait_ge(rx_done, c + 1)
                norm_stats(c, k + 1, st_p, mv_p, rs_p, p_stat, p_var, p_eps)

            def p_norm(k):
                if k >= 1:
                    dve.wait_ge(u_lo_done, k)
                norm_apply(k % NCH, k + 1, u, mv_p, rs_p, p_rstd, p_u)

            def p_uT_parts(k):
                dve.wait_ge(uT_done, k + 1)
                dve.tensor_copy(uT_hi[:, :], uT[:, :]).then_inc(uT_hi_done, 1)
                dve.wait_ge(uT_hi_done, k + 1)
                dve.tensor_tensor(uT_lo[:, :], uT[:, :], uT_hi[:, :].bitcast(F32), ALU.subtract).then_inc(uT_lo_done, 1)

            def p_q_lo(k):
                dve.wait_ge(q_hi_done, k + 1)
                dve.scalar_tensor_tensor(out=qT_lo[:, :], in0=p_ps[1][:, :], scalar=pcol[:, COL_BQ:COL_BQ + 1],
                                         in1=qT_hi[:, :].bitcast(F32), op0=ALU.add, op1=ALU.subtract).then_inc(q_lo_done, 1)

            def p_k_lo(k):
                dve.wait_ge(k_hi_done, k + 1)
                dve.scalar_tensor_tensor(out=kT_lo[:, :], in0=p_ps[0][:, :], scalar=pcol[:, COL_BK:COL_BK + 1],
                                         in1=kT_hi[:, :].bitcast(F32), op0=ALU.add, op1=ALU.subtract).then_inc(k_lo_done, 1)

            def p_attnT_lo(k, b):
                dve.wait_ge(at_hi_done, NB * k + b + 1)
                dve.tensor_tensor(attnT_lo[:, b, :, :].rearrange("p a s -> p (a s)"), p_ps[1 - b][:, :],
                                  attnT_hi[:, b, :, :].rearrange("p a s -> p (a s)").bitcast(F32),
                                  ALU.subtract).then_inc(at_lo_done, 1)

            def p_context_lo(k):
                dve.wait_ge(c_hi_done, k + 1)
                dve.tensor_tensor(cT_lo[:, :], p_ps[1][:, :], cT_hi[:, :].bitcast(F32), ALU.subtract).then_inc(c_lo_done, 1)

            def p_max(k, b):
                dve.wait_ge(sc_ready, NB * k + b + 1)
                dve.tensor_reduce(smx[:, b, :], p_ps[1 - b][:, :].rearrange("p (i s) -> p i s", i=2),
                                  AX_X, ALU.max).then_inc(smx_done, 1)
                dve.wait_ge(smx_done, NB * k + b + 1)
                dve.tensor_scalar(nmx[:, b, :], smx[:, b, :], -SCALE, None, ALU.mult).then_inc(nmx_done, 1)

            def p_attn(k, b):
                dve.wait_ge(exp_done, NB * k + b + 1)
                dve.reciprocal(rsum[:, b, :], esum[:, b, :]).then_inc(rsum_done, 1)
                dve.wait_ge(rsum_done, NB * k + b + 1)
                for i in range(2):
                    last = dve.tensor_scalar(attn[:, b, i, :], ex[:, b, i, :], rsum[:, b, i:i + 1], None, ALU.mult)
                last.then_inc(attn_done, 1)

            def p_z(k):
                par = k % 2
                dve.wait_ge(a_ready, k + 1)
                if k == 0:
                    dve.wait_ge(bvo_done, 1)
                dve.scalar_tensor_tensor(out=facc[:, par, :], in0=p_ps[0][:, :], scalar=bvo[:, 0:1],
                                         in1=uT[:, :], op0=ALU.add, op1=ALU.add).then_inc(z_done, 1)
                dve.wait_ge(z_done, k + 1)
                dve.tensor_copy(zhi[:, par, :], facc[:, par, :]).then_inc(zhi_done, 1)

            def p_zlo(k):
                par = k % 2
                dve.wait_ge(zhi_done, k + 1)
                dve.tensor_tensor(zlo[:, par, :], facc[:, par, :], zhi[:, par, :].bitcast(F32),
                                  ALU.subtract).then_inc(zlo_done, 1)

            def p_gate_shift(k):
                dve.wait_ge(lg_ready, k + 1)
                dve.tensor_tensor(lg[:, :, :], p_ps[1][:, 0:TL * NE].rearrange("p (t e) -> p t e", t=TL),
                                  pcol[:, COL_BG:COL_BG + NE].unsqueeze(1).to_broadcast([P, TL, NE]), ALU.add).then_inc(lg_done, 1)
                dve.wait_ge(lg_done, k + 1)
                dve.tensor_reduce(lmx[:, :], lg[:, :, :], AX_X, ALU.max).then_inc(lmx_done, 1)
                dve.wait_ge(lmx_done, k + 1)
                dve.tensor_tensor(lsh[:, :, :], lg[:, :, :], lmx[:, :].unsqueeze(2).to_broadcast([P, TL, NE]),
                                  ALU.subtract).then_inc(lsh_done, 1)

            def p_gate_norm(k):
                dve.wait_ge(lex_done, k + 1)
                dve.tensor_reduce(lsm[:, :], lex[:, :, :], AX_X, ALU.add).then_inc(lsm_done, 1)
                dve.wait_ge(lsm_done, k + 1)
                dve.reciprocal(lrc[:, :], lsm[:, :]).then_inc(lrc_done, 1)
                dve.wait_ge(lrc_done, k + 1)
                dve.tensor_tensor(gts[:, :, :], lex[:, :, :], lrc[:, :].unsqueeze(2).to_broadcast([P, TL, NE]),
                                  ALU.mult).then_inc(gts_done, 1)

            def fold(j):
                dve.wait_ge(fold_ready, j + 1)
                rows = rows_of(j % NCH)
                dve.scalar_tensor_tensor(out=rows, in0=r_ps[:, :].rearrange("p (t h) -> p t h", t=TL),
                                         scalar=0.5, in1=rows, op0=ALU.mult, op1=ALU.add).then_inc(fold_done, 1)

            def r_norm_stats(c):
                dve.wait_ge(fold_done, c + 1)
                norm_stats(c, c + 1, st_r, mv_r, rs_r, r_stat, r_var, r_eps)

            def r_norm(c):
                if c == 0:
                    dve.wait_ge(wlo_done, 2 * NE)
                norm_apply(c, c + 1, v, mv_r, rs_r, r_rstd, r_v)

            def r_decay(c, b):
                dve.wait_ge(rsc_ready, NB * c + b + 1)
                dve.wait_ge(dmask_done, 1)
                dve.tensor_tensor(pT[:, b, :], r_ps[:, 0:384], dmask, ALU.mult).then_inc(pT_done, 1)

            def r_add(c):
                dve.wait_ge(r_ready, c + 1)
                rows = rows_of(c)
                dve.scalar_tensor_tensor(out=rows, in0=r_ps[:, :].rearrange("p (t h) -> p t h", t=TL),
                                         scalar=pcol[:, COL_OSCALE:COL_OSCALE + 1], in1=rows, op0=ALU.mult, op1=ALU.add
                                         ).then_inc(rx_done, 1)

            dve.wait_ge(x0_in, 16)
            p_norm_stats(0)
            p_norm(0)
            p_uT_parts(0)
            dve.wait_ge(params_in, 16)
            p_q_lo(0)
            p_k_lo(0)
            dve.wait_ge(bvo_ready, 1)
            dve.tensor_tensor(bvo[:, :], down_ps[1][:, 0:1], pcol[:, COL_BO:COL_BO + 1], ALU.add).then_inc(bvo_done, 1)
            for b in range(NB):
                p_max(0, b)
            for b in range(NB):
                p_attn(0, b)
            for b in range(NB):
                p_attnT_lo(0, b)
            p_context_lo(0)
            p_z(0)
            p_zlo(0)
            dve.tensor_scalar(dcy[:, 1:2], pcol[:, COL_DECAY:COL_DECAY + 1], -1.0, None, ALU.mult).then_inc(dcy_vec, 1)
            dve.wait_ge(dcy_vec, 1)
            dve.tensor_tensor(dcy[:, 2:3], pcol[:, COL_DECAY:COL_DECAY + 1], dcy[:, 1:2], ALU.max).then_inc(dcy_vec, 1)
            dve.tensor_scalar(dcy[:, 5:6], pcol[:, COL_DECAY:COL_DECAY + 1], 0.0, None, ALU.min).then_inc(dcy_vec, 1)

            for j in range(PHASES):
                k = j + 1
                for n in range(UNITS):
                    if j == 0 and n == 0:
                        p_gate_shift(0)
                    if j == 0 and n == 1:
                        p_gate_norm(0)
                    if j >= 1:
                        if n == AT_FOLD:
                            fold(j - 1)
                        if j <= NCH:
                            if n == AT_RNORM:
                                r_norm_stats(j - 1)
                            if n == AT_RNORM + 2:
                                r_norm(j - 1)
                            if n in AT_RSC:
                                r_decay(j - 1, AT_RSC.index(n))
                            if n == AT_R:
                                r_add(j - 1)
                    at = side_unit(j, n)
                    if k < PHASES:
                        if at == AT_NORM:
                            p_norm_stats(k)
                        if at == AT_NORM + 2:
                            p_norm(k)
                        if at == AT_UT:
                            p_uT_parts(k)
                        if at == AT_Q:
                            p_q_lo(k)
                        if at == AT_K:
                            p_k_lo(k)
                        if at in AT_AT:
                            p_attnT_lo(k, AT_AT.index(at))
                        if at == AT_C:
                            p_context_lo(k)
                        if at in AT_SC:
                            p_max(k, AT_SC.index(at))
                        if at - 1 in AT_SC:
                            p_attn(k, AT_SC.index(at - 1))
                        if at == AT_A:
                            p_z(k)
                        if at == AT_A + 1:
                            p_zlo(k)
                        if at == AT_LG:
                            p_gate_shift(k)
                        if at == AT_LG + 1:
                            p_gate_norm(k)
                    if j == 0 and n == 26:
                        dve.wait_ge(dcy_act, 2)
                        dve.wait_ge(dcy_vec, 3)
                        dve.tensor_tensor(dcy[:, 6:7], dcy[:, 5:6], dcy[:, 4:5], ALU.subtract).then_inc(dcy_vec, 1)
                    if j == 0 and n == 29:
                        dve.wait_ge(dcy_act, 3)
                        dve.tensor_tensor(dmask, dmask, shp[:, 0, :], ALU.mult).then_inc(dmask_done, 1)
                    if not HI_ON_ACT[n]:
                        hi(j, n)
                    lo(j, n)
                    m = n - LAG - 1
                    if m >= 0 and m % DQ == DQ - 1:
                        gate(j, m // DQ)
                    elif m < 0 and (m + UNITS) % DQ == DQ - 1 and j >= 1:
                        gate(j - 1, NE - 1)
            gate(PHASES - 1, NE - 1)
            fold(PHASES - 1)

        @block.gpsimd
        def _(pool):
            def rstd(count, rs, eps, done):
                pool.wait_ge(eps, count)
                pool.tensor_tensor(rs[:, 1, :], rs[:, 0, :], mhalf[:, :], ALU.pow).then_inc(done, 1)

            def u_low(k):
                pool.wait_ge(u_hi_done, k + 1)
                pool.tensor_tensor(u_lo[:, :, :], u[:, :, :], u_hi[:, :, :].bitcast(F32), ALU.subtract
                                   ).then_inc(u_lo_done, 1)

            def split_w_lo(e):
                pool.wait_ge(whi_done, 2 * e + 1)
                pool.tensor_tensor(w1lo[:, e, :], wraw[:, e % NWR, 0, :], w1hi[:, e, :].bitcast(F32), ALU.subtract
                                   ).then_inc(wlo_done, 1)
                pool.wait_ge(whi_done, 2 * e + 2)
                pool.tensor_tensor(w2lo[:, e, :], wraw[:, e % NWR, 1, :], w2hi[:, e, :].bitcast(F32), ALU.subtract
                                   ).then_inc(wlo_done, 1)

            def add(j, e):
                G = NE * j + e
                pool.wait_ge(gate_done, G + 1)
                if G >= 1:
                    pool.wait_ge(sum_done, G)
                acc = facc[:, j % 2, :]
                pool.tensor_tensor(acc, acc, gated[:, e % 2, :], ALU.add).then_inc(sum_done, 1)

            pool.memset(mhalf[:, :], -0.5).then_inc(mhalf_set, 1)
            pool.wait_ge(mhalf_set, 1)
            rstd(1, rs_p, p_eps, p_rstd)
            pool.wait_ge(wqk_hi_done, 1)
            pool.tensor_tensor(wqk_lo[:, :, :].rearrange("p a h -> p (a h)"), wattn[:, 0:2 * P],
                               wqk_hi[:, :, :].rearrange("p a h -> p (a h)").bitcast(F32), ALU.subtract
                               ).then_inc(wqk_lo_done, 1)
            u_low(0)
            pool.wait_ge(wvo_hi_done, 1)
            pool.tensor_tensor(wvo_lo[:, :], wvo[:, :], wvo_hi[:, :].bitcast(F32), ALU.subtract
                               ).then_inc(wvo_lo_done, 1)
            split_w_lo(0)
            split_w_lo(1)
            for j in range(PHASES):
                if j + 1 < PHASES:
                    rstd(j + 2, rs_p, p_eps, p_rstd)
                if j >= 1:
                    add(j - 1, NE - 1)
                    if j <= NCH:
                        rstd(j, rs_r, r_eps, r_rstd)
                for e in range(NE - 1):
                    if j == 0 and e + 2 < NE:
                        split_w_lo(e + 2)
                    add(j, e)
                    if e == 0 and j + 1 < PHASES:
                        u_low(j + 1)
            add(PHASES - 1, NE - 1)


SCALE = float(P) ** -0.5


def kernel(**inputs):
    import numpy as np
    import concourse.bacc as bacc
    from concourse.bass_utils import run_bass_kernel_spmd as run

    def ffn(name):
        return np.asarray(inputs["L0_ffn_" + name])

    def attn(name):
        return np.asarray(inputs["L0_attn_" + name])

    x = attn("x")
    x_rows = np.ascontiguousarray(x.reshape(-1, P, P).transpose(1, 0, 2))
    w1 = ffn("W1").transpose(1, 0, 2)
    w2 = ffn("W2").reshape(NE, DQ, P, P).transpose(2, 0, 1, 3).reshape(P, NE, CH)
    experts = np.ascontiguousarray(np.stack([w1, w2], axis=2))
    attn_weights = np.concatenate([ffn("Wq"), ffn("Wk"), ffn("Wv").T, ffn("Wo"), ffn("Wg")], axis=1)
    vectors = [ffn("b1").reshape(NE * DQ, P), ffn("b2")]
    vectors += [a.reshape(1, P) for a in (ffn("bq"), ffn("bk"), ffn("bv"), ffn("bo"),
                                          attn("q_scale"), attn("k_scale"))]
    everywhere = [attn("decay_logit").reshape(1), attn("out_scale").reshape(1), ffn("bg")]
    params = np.concatenate([np.concatenate(vectors).T,
                             np.broadcast_to(np.concatenate(everywhere), (P, 2 + NE))], axis=1)

    s = np.arange(P)[:, None]
    diff = np.concatenate([s - np.arange(P)[None, :], s + P - np.arange(SEQ)[None, :]], axis=1)
    decay_shapes = np.stack([diff > 0, np.maximum(diff - 1, 0)], axis=1).astype(np.float32)

    nc = bacc.Bacc("TRN2", target_bir_lowering=False, num_devices=1)
    arrays = {"x_rows": x_rows, "experts": experts, "attn_weights": attn_weights, "params": params,
              "identity": np.eye(P, dtype=np.float32), "decay_shapes": decay_shapes}
    arrays = {name: np.ascontiguousarray(a) for name, a in arrays.items()}
    args = [nc.dram_tensor(name, a.shape, mybir.dt.from_np(a.dtype), kind="ExternalInput").ap()
            for name, a in arrays.items()]
    args.append(nc.dram_tensor("gates_scratch", (2, NE, CH), F32, kind="Internal").ap())
    args.append(nc.dram_tensor("out_rows", x_rows.shape, F32, kind="ExternalOutput").ap())
    macaron(nc, *args)
    r = run(nc, [arrays], core_ids=[0])
    return r.results[0]["out_rows"].transpose(1, 0, 2).reshape(x.shape)
```

```python
from contextlib import ExitStack

import concourse.bass as bass
from concourse import mybir

F32 = mybir.dt.float32
F32R = mybir.dt.float32r
ALU = mybir.AluOpType
ACT = mybir.ActivationFunctionType
AX_X = mybir.AxisListType.X

P = 128
NCH = 4
CH = 512
TL = CH // P
SEQ = 256
NB = CH // SEQ
NE = 8
DQ = 4
UNITS = NE * DQ
PHASES = 2 * NCH
EPS = 1e-5

LAG = 3
NU = 3
WARM = 7
NWR = 4
NHF = 3
NHS = 4
FIRST_GATES = 2

COL_B1, COL_B2 = 0, 32
COL_BQ, COL_BK, COL_BV, COL_BO, COL_QS, COL_KS, COL_DECAY, COL_OSCALE = range(40, 48)
COL_BG = 48
NCOLS = COL_BG + NE
NATTN = 4 * P + NE

AT_NORM = 0
AT_UT = 4
AT_Q = 6
AT_K = 6
AT_SC = (9, 11)
AT_AT = (13, 15)
AT_C = 18
AT_A = 20
AT_LG = 24
AT_GT = 31
AT_FOLD = 7
AT_RNORM = 10
AT_VT = 14
AT_RSC = (17, 22)
AT_R = 24

AT0_LG = (0, 7)
AT0_GT = (3, 11)
AT0_AT = (1, 2)
AT0_C = 3

HI_ON_ACT = [n not in (2, 14, 16, 19, 21, 27, 28, 31) for n in range(UNITS)]
HI_ON_ACT_0 = [n not in (1, 2, 4, 5, 7, 9, 11, 14, 17, 19, 20, 21, 24, 26, 27, 28, 30) for n in range(UNITS)]
END_GATE = 30
SPLIT_W_AT = (2, 4, 6, 13, 15, 20)


def macaron(nc, x, experts, attn_weights, params, identity, decay_shapes, gates_dram, out):
    ctx = ExitStack()
    with ctx:
        def sb(name, shape, dt=F32):
            return ctx.enter_context(nc.sbuf_tensor(name, shape, dt))

        def bank(name):
            return ctx.enter_context(nc.psum_tensor(name, [P, 512], F32))

        def sem(name):
            return ctx.enter_context(nc.semaphore(name))

        xs = sb("xs", [P, NCH * TL, P])
        wraw = sb("wraw", [P, NWR, 2, CH])
        v = wraw[:, 0, 0, :].rearrange("p (t h) -> p t h", t=TL)
        rqT = wraw[:, 0, 1, :]
        rkT = wraw[:, 1, 0, :]
        pT = wraw[:, 2, :, 0:384]
        w1hi = sb("w1hi", [P, NE, CH], F32R)
        w1lo = sb("w1lo", [P, NE, CH], F32R)
        w2hi = sb("w2hi", [P, NE, CH], F32R)
        w2lo = sb("w2lo", [P, NE, CH], F32R)
        wattn = sb("wattn", [P, NATTN])
        wq, wk, wvT, wo = (wattn[:, i * P:(i + 1) * P] for i in range(4))
        wg = wattn[:, 4 * P:NATTN]
        wqk_hi = sb("wqk_hi", [P, 2, P], F32R)
        wqk_lo = sb("wqk_lo", [P, 2, P], F32R)
        wvo = sb("wvo", [P, P])
        wvo_hi = sb("wvo_hi", [P, P], F32R)
        wvo_lo = sb("wvo_lo", [P, P], F32R)
        bvo = sb("bvo", [P, 1])
        pcol = sb("pcol", [P, NCOLS])
        ident_t = sb("ident_t", [P, P])
        ident = ident_t[:, :]
        shp = sb("shp", [P, 2, 384])
        dcy = sb("dcy", [P, 8])
        dmask = shp[:, 1, :]
        mhalf = sb("mhalf", [P, TL])
        u = sb("u", [P, TL, P])
        st_p = sb("st_p", [P, 2, TL, 6])
        mv_p = sb("mv_p", [P, 2, TL, 2])
        rs_p = sb("rs_p", [P, 2, 2, TL])
        st_r = sb("st_r", [P, TL, 6])
        mv_r = sb("mv_r", [P, TL, 2])
        rs_r = sb("rs_r", [P, 2, TL])
        uT = sb("uT", [P, CH])
        u_hi = sb("u_hi", [P, TL, P], F32R)
        u_lo = sb("u_lo", [P, TL, P], F32R)
        uT_hi = sb("uT_hi", [P, CH], F32R)
        uT_lo = sb("uT_lo", [P, CH], F32R)
        qT_hi = sb("qT_hi", [P, CH], F32R)
        qT_lo = sb("qT_lo", [P, CH], F32R)
        kT_hi = sb("kT_hi", [P, CH], F32R)
        kT_lo = sb("kT_lo", [P, CH], F32R)
        smx = sb("smx", [P, 2, NB, 2])
        nmx = sb("nmx", [P, 2, NB, 2])
        esum = sb("esum", [P, 2, NB, 2])
        rsum = sb("rsum", [P, 2, NB, 2])
        ex = sb("ex", [P, NB, 2, SEQ])
        attnT_hi = sb("attnT_hi", [P, NB, 2, SEQ], F32R)
        attnT_lo = sb("attnT_lo", [P, NB, 2, SEQ], F32R)
        cT_hi = sb("cT_hi", [P, CH], F32R)
        cT_lo = sb("cT_lo", [P, CH], F32R)
        facc = sb("facc", [P, 2, CH])
        zhi = sb("zhi", [P, 2, CH], F32R)
        zlo = sb("zlo", [P, 2, CH], F32R)
        lg = sb("lg", [P, TL, NE])
        lmx = sb("lmx", [P, TL])
        lsh = sb("lsh", [P, TL, NE])
        lex = sb("lex", [P, TL, NE])
        lsm = sb("lsm", [P, TL])
        lrc = sb("lrc", [P, TL])
        gts = sb("gts", [P, NE, TL])
        gT = sb("gT", [NE * TL, P])
        gbc = sb("gbc", [P, 2, NE, CH])
        hF = sb("hF", [P, NHF, CH])
        hhi = sb("hhi", [P, NHS, CH], F32R)
        hlo = sb("hlo", [P, NHS, CH], F32R)
        gated = sb("gated", [P, 2, CH])

        up_ps = [bank(f"up_ps{i}") for i in range(NU)]
        down_ps = [bank(f"down_ps{i}") for i in range(2)]
        p_ps = [bank(f"p_ps{i}") for i in range(2)]
        r_ps = bank("r_ps")

        def side_bank(k, i):
            return ((r_ps, down_ps[1]) if k == 1 else p_ps)[i]

        def early(k, slot):
            return gbc[:, k, slot, :]

        def early_pair(k, slot):
            return gbc[:, k, slot:slot + 2, :].rearrange("p b (i s) -> p b i s", i=2)

        def u_of(k):
            return early(k, 0).rearrange("p (t h) -> p t h", t=TL) if k < 2 else u[:, :, :]

        def uT_of(k):
            return early(k, 1) if k < 2 else uT[:, :]

        def qT_of(k):
            return early(k, 2) if k < 2 else qT_hi[:, :]

        def kT_of(k):
            return early(k, 3) if k < 2 else kT_hi[:, :]

        def ex_of(k):
            return early_pair(k, 4) if k < 2 else ex[:, :, :, :]

        def attnT_of(k):
            return early_pair(k, 6) if k < 2 else attnT_hi[:, :, :, :]

        def values_of(k):
            return early(k, 0).rearrange("p (t h) -> p t h", t=TL)

        x0_in, x1_in = sem("x0_in"), sem("x1_in")
        ident_in = sem("ident_in")
        wattn_in = sem("wattn_in")
        params_in = sem("params_in")
        shapes_in = sem("shapes_in")
        xrest_in = sem("xrest_in")
        w_in = [sem(f"w_in{e}") for e in range(NE)]
        mhalf_set, warm_set = sem("mhalf_set"), sem("warm_set")
        whi_done = sem("whi_done")
        wlo_done = sem("wlo_done")
        wqk_hi_done, wqk_lo_done = sem("wqk_hi_done"), sem("wqk_lo_done")
        wvo_ready, wvo_done = sem("wvo_ready"), sem("wvo_done")
        wvo_hi_done, wvo_lo_done = sem("wvo_hi_done"), sem("wvo_lo_done")
        u_hi_done, u_lo_done = sem("u_hi_done"), sem("u_lo_done")
        bvo_ready, bvo_done = sem("bvo_ready"), sem("bvo_done")
        dcy_vec, dcy_act, dmask_done = sem("dcy_vec"), sem("dcy_act"), sem("dmask_done")
        up_ready, relu_done = sem("up_ready"), sem("relu_done")
        hi_act_done, hi_vec_done, lo_done = sem("hi_act_done"), sem("hi_vec_done"), sem("lo_done")
        down_ready, gate_done, sum_done = sem("down_ready"), sem("gate_done"), sem("sum_done")
        p_stat, p_var, p_eps, p_rstd, p_u = (sem(f"p_{n}") for n in ("stat", "var", "eps", "rstd", "u"))
        r_stat, r_var, r_eps, r_rstd, r_v = (sem(f"r_{n}") for n in ("stat", "var", "eps", "rstd", "v"))
        uT_ready, uT_done = sem("uT_ready"), sem("uT_done")
        uT_hi_done, uT_lo_done = sem("uT_hi_done"), sem("uT_lo_done")
        q_ready, q_done, q_lo_done = sem("q_ready"), sem("q_done"), sem("q_lo_done")
        k_ready, k_done, k_lo_done = sem("k_ready"), sem("k_done"), sem("k_lo_done")
        sc_ready, smx_done, nmx_done = sem("sc_ready"), sem("smx_done"), sem("nmx_done")
        exp_done, rsum_done, attn_done = sem("exp_done"), sem("rsum_done"), sem("attn_done")
        at_ready, at_done, at_lo_done = sem("at_ready"), sem("at_done"), sem("at_lo_done")
        vo_ready, vo_done = sem("vo_ready"), sem("vo_done")
        c_ready, c_done, c_lo_done = sem("c_ready"), sem("c_done"), sem("c_lo_done")
        a_ready, z_done, zhi_done, zlo_done = sem("a_ready"), sem("z_done"), sem("zhi_done"), sem("zlo_done")
        lg_ready, lg_done, lmx_done, lsh_done = sem("lg_ready"), sem("lg_done"), sem("lmx_done"), sem("lsh_done")
        lex_done, lsm_done, lrc_done, gts_done = sem("lex_done"), sem("lsm_done"), sem("lrc_done"), sem("gts_done")
        gT_ready, gT_done = sem("gT_ready"), sem("gT_done")
        gates_out, first_gates_in = sem("gates_out"), sem("first_gates_in")
        gbc_in = [sem(f"gbc_in{i}") for i in range(2)]
        fold_ready, fold_done = sem("fold_ready"), sem("fold_done")
        vT_ready, rqk_done = sem("vT_ready"), sem("rqk_done")
        rsc_ready, pT_done = sem("rsc_ready"), sem("pT_done")
        r_ready, rx_done = sem("r_ready"), sem("rx_done")
        end_gate_done, end_fold_ready, end_fold_done = (sem(f"end_{n}") for n in ("gate_done", "fold_ready", "fold_done"))
        stored = sem("stored")

        def hi_on_act(j, n):
            return (HI_ON_ACT if j else HI_ON_ACT_0)[n]

        def hi_count(j, n, on_act):
            if j == 0:
                return HI_ON_ACT_0[:n + 1].count(on_act)
            return HI_ON_ACT_0.count(on_act) + (j - 1) * HI_ON_ACT.count(on_act) + HI_ON_ACT[:n + 1].count(on_act)

        def rows_of(chunk):
            return xs[:, bass.ds(chunk * TL, TL), :] if not isinstance(chunk, int) else \
                xs[:, chunk * TL:(chunk + 1) * TL, :]

        def row_tile(chunk, t):
            return xs[:, bass.ds(chunk * TL + t, 1), :] if not isinstance(chunk, int) else \
                xs[:, chunk * TL + t, :]

        block = ctx.enter_context(nc.Block())

        @block.sync
        def _(sp):
            sp.dma_start(rows_of(0), x[:, 0:TL, :]).then_inc(x0_in, 16)
            sp.dma_start(ident, identity).then_inc(ident_in, 16)
            sp.dma_start(rows_of(1), x[:, TL:2 * TL, :]).then_inc(x1_in, 16)
            sp.dma_start(pcol[:, :], params).then_inc(params_in, 16)

            def load_expert(e):
                if e >= NWR:
                    sp.wait_ge(wlo_done, 2 * (e - NWR) + 2)
                sp.dma_start(wraw[:, e % NWR, :, :], experts[:, e, :, :]).then_inc(w_in[e], 16)

            def spread_gates(k):
                par = k % 2
                sp.wait_ge(gT_done, k + 1)
                if k >= 2:
                    sp.wait_ge(gbc_in[par], 16 * (k // 2))
                sp.dma_start(gates_dram[par].rearrange("e (t p) -> (e t) p", t=TL), gT[:, :]).then_inc(gates_out, 16)
                sp.wait_ge(gates_out, 16 * (k + 1))
                if k >= 2:
                    sp.wait_ge(gate_done, NE * (k - 1))
                first = 0
                if k == 0:
                    first = FIRST_GATES
                    sp.dma_start(gbc[:, 0, 0:first, :], gates_dram[0:1, 0:first].to_broadcast([P, first, CH])
                                 ).then_inc(first_gates_in, 16)
                sp.dma_start(gbc[:, par, first:, :], gates_dram[par:par + 1, first:].to_broadcast([P, NE - first, CH])
                             ).then_inc(gbc_in[par], 16)

            def store(j):
                c = j % NCH
                sp.wait_ge(fold_done, j + 1)
                sp.dma_start(out[:, c * TL:(c + 1) * TL, :], rows_of(c)).then_inc(stored, 16)

            for e in range(NWR):
                load_expert(e)
            sp.dma_start(xs[:, 2 * TL:, :], x[:, 2 * TL:, :]).then_inc(xrest_in, 16)
            sp.dma_start(shp[:, :, :], decay_shapes).then_inc(shapes_in, 16)
            load_expert(NWR)
            load_expert(NWR + 1)
            spread_gates(0)
            for e in range(NWR + 2, NE):
                load_expert(e)
            for j in range(PHASES):
                if j > NCH:
                    store(j - 1)
                if j + 1 < PHASES:
                    spread_gates(j + 1)
            for b in range(NB):
                tiles = slice((NCH - 1) * TL + 2 * b, (NCH - 1) * TL + 2 * b + 2)
                sp.wait_ge(end_fold_done, b + 1)
                sp.dma_start(out[:, tiles, :], xs[:, tiles, :]).then_inc(stored, 16)
            sp.wait_ge(stored, 16 * (NCH - 1 + NB))

        @block.tensor
        def _(pe):
            def up(j, n):
                e, d = divmod(n, DQ)
                T = UNITS * j + n
                if n == 0:
                    pe.wait_ge(zhi_done, j + 1)
                if j == 0 and d == 0:
                    pe.wait_ge(wlo_done, 2 * e + 1)
                if T >= NU:
                    pe.wait_ge(relu_done, T - NU + 1)
                elif T == 2:
                    pe.wait_ge(vo_done, 2)
                dst = up_ps[T % NU][:, :]
                cols = slice(P * d, P * d + P)
                pe.matmul(dst, w1lo[:, e, cols], zhi[:, j % 2, :], start=True, stop=False)
                pe.matmul(dst, w1hi[:, e, cols], zhi[:, j % 2, :], start=False, stop=False)
                if n == 0:
                    pe.wait_ge(zlo_done, j + 1)
                pe.matmul(dst, w1hi[:, e, cols], zlo[:, j % 2, :], start=False, stop=True).then_inc(up_ready, 1)

            def down(j, n):
                e, d = divmod(n, DQ)
                T = UNITS * j + n
                if j == 0 and d == 0:
                    pe.wait_ge(wlo_done, 2 * e + 2)
                G = NE * j + e
                if d == 0 and G >= 2:
                    pe.wait_ge(gate_done, G - 1)
                elif d == 0 and G == 1:
                    pe.wait_ge(z_done, 2)
                elif d == 0:
                    pe.wait_ge(bvo_done, 1)
                pe.wait_ge(hi_act_done if hi_on_act(j, n) else hi_vec_done, hi_count(j, n, hi_on_act(j, n)))
                dst = down_ps[e % 2][:, :]
                cols = slice(P * d, P * d + P)
                h = T % NHS
                pe.matmul(dst, w2lo[:, e, cols], hhi[:, h, :], start=(d == 0), stop=False)
                pe.matmul(dst, w2hi[:, e, cols], hhi[:, h, :], start=False, stop=False)
                pe.wait_ge(lo_done, T + 1)
                pe.matmul(dst, w2hi[:, e, cols], hlo[:, h, :], start=False, stop=(d == DQ - 1)
                          ).then_inc(down_ready, 1)

            def transpose_tiles(dst, src_of, done, rows_done=None, before=0):
                for t in range(TL):
                    if rows_done:
                        pe.wait_ge(rows_done, before + t + 1)
                    last = pe.transpose(dst[:, t * P:(t + 1) * P], src_of(t), ident)
                last.then_inc(done, 1)

            def p_uT(k):
                if k >= 2:
                    pe.wait_ge(gT_done, k)
                transpose_tiles(side_bank(k, 0), lambda t: u_of(k)[:, t, :], uT_ready, p_u, TL * k)

            def p_q(k):
                dst = side_bank(k, 1)[:, :]
                if k < 2:
                    pe.wait_ge(uT_done, k + 1)
                    pe.matmul(dst, wq, uT_of(k), start=True, stop=True).then_inc(q_ready, 1)
                    return
                if k == 2:
                    pe.wait_ge(wqk_lo_done, 1)
                pe.wait_ge(uT_hi_done, k - 1)
                pe.matmul(dst, wqk_lo[:, 0, :], uT_hi[:, :], start=True, stop=False)
                pe.matmul(dst, wqk_hi[:, 0, :], uT_hi[:, :], start=False, stop=False)
                pe.wait_ge(uT_lo_done, k - 1)
                pe.matmul(dst, wqk_hi[:, 0, :], uT_lo[:, :], start=False, stop=True).then_inc(q_ready, 1)

            def p_k(k):
                dst = side_bank(k, 0)[:, :]
                if k < 2:
                    pe.matmul(dst, wk, uT_of(k), start=True, stop=True).then_inc(k_ready, 1)
                    return
                pe.matmul(dst, wqk_lo[:, 1, :], uT_hi[:, :], start=True, stop=False)
                pe.matmul(dst, wqk_hi[:, 1, :], uT_hi[:, :], start=False, stop=False)
                pe.matmul(dst, wqk_hi[:, 1, :], uT_lo[:, :], start=False, stop=True).then_inc(k_ready, 1)

            def p_scores(k, b):
                if k < 2:
                    pe.wait_ge(q_done, k + 1)
                    pe.wait_ge(k_done, k + 1)
                else:
                    pe.wait_ge(q_lo_done, k - 1)
                    pe.wait_ge(k_lo_done, k - 1)
                keys = slice(b * SEQ, (b + 1) * SEQ)
                for i in range(2):
                    dst = side_bank(k, 1 - b)[:, i * SEQ:(i + 1) * SEQ]
                    qs = slice(b * SEQ + i * P, b * SEQ + (i + 1) * P)
                    if k < 2:
                        last = pe.matmul(dst, qT_of(k)[:, qs], kT_of(k)[:, keys], start=True, stop=True)
                    else:
                        pe.matmul(dst, qT_lo[:, qs], kT_hi[:, keys], start=True, stop=False)
                        pe.matmul(dst, qT_hi[:, qs], kT_hi[:, keys], start=False, stop=False)
                        last = pe.matmul(dst, qT_hi[:, qs], kT_lo[:, keys], start=False, stop=True)
                last.then_inc(sc_ready, 1)

            def p_attnT(k, b):
                pe.wait_ge(attn_done, NB * k + b + 1)
                for kt in range(2):
                    for i in range(2):
                        at = kt * SEQ + i * P
                        last = pe.transpose(side_bank(k, 1 - b)[:, at:at + P],
                                            ex_of(k)[:, b, i, kt * P:(kt + 1) * P], ident)
                last.then_inc(at_ready, 1)

            def p_values(k):
                pe.wait_ge(wvo_done, 1)
                for t in range(TL):
                    last = pe.matmul(up_ps[1 + k][:, t * P:(t + 1) * P], uT_of(k)[:, t * P:(t + 1) * P], wvo[:, :],
                                     start=True, stop=True)
                last.then_inc(vo_ready, 1)

            def p_early_context(k):
                pe.wait_ge(vo_done, k + 1)
                for b in range(NB):
                    pe.wait_ge(at_done, NB * k + b + 1)
                    for kt in range(2):
                        last = pe.matmul(side_bank(k, 1)[:, b * SEQ:(b + 1) * SEQ], values_of(k)[:, 2 * b + kt, :],
                                         attnT_of(k)[:, b, kt, :], start=(kt == 0), stop=(kt == 1))
                last.then_inc(a_ready, 1)

            def p_context(k):
                pe.wait_ge(u_lo_done, k - 1)
                for b in range(NB):
                    pe.wait_ge(at_lo_done, NB * (k - 2) + b + 1)
                    dst = side_bank(k, 1)[:, b * SEQ:(b + 1) * SEQ]
                    for kt in range(2):
                        t = 2 * b + kt
                        pe.matmul(dst, u_lo[:, t, :], attnT_hi[:, b, kt, :], start=(kt == 0), stop=False)
                        pe.matmul(dst, u_hi[:, t, :], attnT_hi[:, b, kt, :], start=False, stop=False)
                        last = pe.matmul(dst, u_hi[:, t, :], attnT_lo[:, b, kt, :], start=False, stop=(kt == 1))
                last.then_inc(c_ready, 1)

            def p_project(k):
                if k == 2:
                    pe.wait_ge(wvo_lo_done, 1)
                pe.wait_ge(c_done, k - 1)
                dst = side_bank(k, 0)[:, :]
                pe.matmul(dst, wvo_lo[:, :], cT_hi[:, :], start=True, stop=False)
                pe.matmul(dst, wvo_hi[:, :], cT_hi[:, :], start=False, stop=False)
                pe.wait_ge(c_lo_done, k - 1)
                pe.matmul(dst, wvo_hi[:, :], cT_lo[:, :], start=False, stop=True).then_inc(a_ready, 1)

            def p_logits(k):
                pe.wait_ge(z_done, k + 1)
                for t in range(TL):
                    last = pe.matmul(p_ps[1][:, t * NE:(t + 1) * NE], facc[:, k % 2, t * P:(t + 1) * P],
                                     wg, start=True, stop=True)
                last.then_inc(lg_ready, 1)

            def p_gatesT(k):
                pe.wait_ge(gts_done, k + 1)
                if k == 1:
                    pe.wait_ge(gT_done, 1)
                pe.transpose(p_ps[0][0:NE * TL, 0:P], gts[:, :, :].rearrange("p e t -> p (e t)"), ident).then_inc(gT_ready, 1)

            def fold(j):
                pe.wait_ge(sum_done, NE * (j + 1) - (j == PHASES - 1))
                if 1 <= j <= NCH:
                    pe.wait_ge(rx_done, j)
                elif j > NCH:
                    pe.wait_ge(fold_done, j)
                transpose_tiles(r_ps, lambda t: facc[:, j % 2, t * P:(t + 1) * P], fold_ready)

            def r_vT(c):
                transpose_tiles(r_ps, lambda t: v[:, t, :], vT_ready, r_v, TL * c)

            def r_scores(c, b):
                pe.wait_ge(rqk_done, c + 1)
                if b:
                    pe.wait_ge(pT_done, NB * c + b)
                o = b * SEQ
                pe.matmul(r_ps[:, 0:P], rkT[:, o:o + P], rqT[:, o:o + P], start=True, stop=True)
                pe.matmul(r_ps[:, P:P + SEQ], rkT[:, o + P:o + SEQ], rqT[:, o:o + SEQ],
                          start=True, stop=True).then_inc(rsc_ready, 1)

            def r_retrieve(c):
                pe.wait_ge(pT_done, NB * (c + 1))
                for b in range(NB):
                    t0 = r_ps[:, (2 * b) * P:(2 * b + 1) * P]
                    t1 = r_ps[:, (2 * b + 1) * P:(2 * b + 2) * P]
                    pe.matmul(t0, pT[:, b, 0:P], v[:, 2 * b, :], start=True, stop=False)
                    pe.matmul(t0, pT[:, b, P:2 * P], v[:, 2 * b + 1, :], start=False, stop=True)
                    last = pe.matmul(t1, pT[:, b, 2 * P:3 * P], v[:, 2 * b + 1, :], start=True, stop=True)
                last.then_inc(r_ready, 1)

            pe.wait_ge(warm_set, 1)
            for _ in range(WARM):
                pe.matmul(up_ps[0][:, 0:SEQ], hF[:, 0, 0:P], hF[:, 0, 0:SEQ], start=True, stop=True)
            pe.wait_ge(ident_in, 16)
            p_uT(0)
            pe.wait_ge(wattn_in, 16)
            pe.matmul(up_ps[0][:, 0:P], wvT, wo, start=True, stop=True).then_inc(wvo_ready, 1)
            p_q(0)
            p_k(0)
            p_values(0)
            p_uT(1)
            p_scores(0, 0)
            p_scores(0, 1)
            p_q(1)
            p_k(1)
            pe.wait_ge(params_in, 16)
            pe.matmul(down_ps[0][:, 0:1], wo, pcol[:, COL_BV:COL_BV + 1], start=True, stop=True
                      ).then_inc(bvo_ready, 1)
            p_attnT(0, 0)
            p_attnT(0, 1)
            p_early_context(0)
            p_scores(1, 0)
            p_scores(1, 1)
            p_values(1)

            for j in range(PHASES):
                for n in range(UNITS):
                    up(j, n)
                    if n >= LAG:
                        down(j, n - LAG)
                    elif j >= 1:
                        down(j - 1, UNITS + n - LAG)
                    if j == 0:
                        if n in AT0_AT:
                            p_attnT(1, AT0_AT.index(n))
                        if n == AT0_C:
                            p_early_context(1)
                        if n in AT0_LG:
                            p_logits(AT0_LG.index(n))
                        if n in AT0_GT:
                            p_gatesT(AT0_GT.index(n))
                    if j >= 1:
                        if n == AT_FOLD:
                            fold(j - 1)
                        if j <= NCH:
                            if n == AT_VT:
                                r_vT(j - 1)
                            if n in AT_RSC:
                                r_scores(j - 1, AT_RSC.index(n))
                            if n == AT_R:
                                r_retrieve(j - 1)
                    k = j + 1
                    if 2 <= k < PHASES:
                        if n == AT_UT:
                            p_uT(k)
                        if n == AT_Q:
                            p_q(k)
                        if n == AT_K:
                            p_k(k)
                        if n in AT_SC:
                            p_scores(k, AT_SC.index(n))
                        if n in AT_AT:
                            p_attnT(k, AT_AT.index(n))
                        if n == AT_C:
                            p_context(k)
                        if n == AT_A:
                            p_project(k)
                        if n == AT_LG:
                            p_logits(k)
                        if n == AT_GT:
                            p_gatesT(k)
            for n in range(UNITS - LAG, UNITS):
                if n == UNITS - 1:
                    fold(PHASES - 1)
                down(PHASES - 1, n)
            for b in range(NB):
                pe.wait_ge(end_gate_done, b + 1)
                for t in (2 * b, 2 * b + 1):
                    last = pe.transpose(p_ps[b][:, (t - 2 * b) * P:(t - 2 * b + 1) * P],
                                        gated[:, (NE - 1) % 2, t * P:(t + 1) * P], ident)
                last.then_inc(end_fold_ready, 1)

        @block.scalar
        def _(act):
            act.dma_start(wattn[:, :], attn_weights).then_inc(wattn_in, 16)

            def relu(j, n):
                T = UNITS * j + n
                act.wait_ge(up_ready, T + 1)
                if T >= NHF:
                    act.wait_ge(lo_done, T - NHF + 1)
                act.activation(hF[:, T % NHF, :], up_ps[T % NU][:, :], ACT.Relu,
                               bias=pcol[:, COL_B1 + n:COL_B1 + n + 1]).then_inc(relu_done, 1)

            def hi(j, n):
                T = UNITS * j + n
                act.wait_ge(up_ready, T + 1)
                if T >= NHS:
                    act.wait_ge(down_ready, T - NHS + 1)
                act.activation(hhi[:, T % NHS, :], up_ps[T % NU][:, :], ACT.Relu,
                               bias=pcol[:, COL_B1 + n:COL_B1 + n + 1]).then_inc(hi_act_done, 1)

            def split_w_hi(e):
                act.wait_ge(w_in[e], 16)
                act.copy(w1hi[:, e, :], wraw[:, e % NWR, 0, :]).then_inc(whi_done, 1)
                act.copy(w2hi[:, e, :], wraw[:, e % NWR, 1, :]).then_inc(whi_done, 1)

            def p_uT(k):
                act.wait_ge(uT_ready, k + 1)
                if k >= 3:
                    act.wait_ge(z_done, k)
                act.copy(uT_of(k), side_bank(k, 0)[:, :]).then_inc(uT_done, 1)

            def p_u_hi(k):
                act.wait_ge(p_u, TL * (k + 1))
                if k >= 3:
                    act.wait_ge(c_ready, k - 2)
                act.copy(u_hi[:, :, :], u[:, :, :]).then_inc(u_hi_done, 1)

            def p_q(k):
                act.wait_ge(q_ready, k + 1)
                act.activation(qT_of(k), side_bank(k, 1)[:, :], ACT.Identity, bias=pcol[:, COL_BQ:COL_BQ + 1]
                               ).then_inc(q_done, 1)

            def p_k(k):
                act.wait_ge(k_ready, k + 1)
                act.activation(kT_of(k), side_bank(k, 0)[:, :], ACT.Identity, bias=pcol[:, COL_BK:COL_BK + 1]
                               ).then_inc(k_done, 1)

            def p_exp(k, b):
                act.wait_ge(nmx_done, NB * k + b + 1)
                if k >= 3:
                    act.wait_ge(attn_done, NB * (k - 1) + b + 1)
                for i in range(2):
                    last = act.activation(ex_of(k)[:, b, i, :], side_bank(k, 1 - b)[:, i * SEQ:(i + 1) * SEQ], ACT.Exp,
                                          bias=nmx[:, k % 2, b, i:i + 1], scale=SCALE,
                                          accum_out=esum[:, k % 2, b, i:i + 1])
                last.then_inc(exp_done, 1)

            def p_attnT(k, b):
                act.wait_ge(at_ready, NB * k + b + 1)
                act.copy(attnT_of(k)[:, b, :, :].rearrange("p a s -> p (a s)"), side_bank(k, 1 - b)[:, :]
                         ).then_inc(at_done, 1)

            def p_context(k):
                act.wait_ge(c_ready, k - 1)
                act.copy(cT_hi[:, :], side_bank(k, 1)[:, :]).then_inc(c_done, 1)

            def p_values(k):
                act.wait_ge(vo_ready, k + 1)
                act.copy(early(k, 0), up_ps[1 + k][:, :]).then_inc(vo_done, 1)

            def p_gate_exp(k):
                act.wait_ge(lsh_done, k + 1)
                act.activation(lex[:, :, :], lsh[:, :, :], ACT.Exp).then_inc(lex_done, 1)

            def p_gatesT(k):
                act.wait_ge(gT_ready, k + 1)
                if k >= 1:
                    act.wait_ge(gates_out, 16 * k)
                act.copy(gT[:, :], p_ps[0][0:NE * TL, 0:P]).then_inc(gT_done, 1)

            def r_qk(c):
                act.wait_ge(vT_ready, c + 1)
                act.activation(rqT, r_ps[:, :], ACT.Copy, scale=pcol[:, COL_QS:COL_QS + 1])
                act.activation(rkT, r_ps[:, :], ACT.Copy, scale=pcol[:, COL_KS:COL_KS + 1]
                               ).then_inc(rqk_done, 1)

            def split_wvo_hi():
                act.wait_ge(wvo_done, 1)
                act.copy(wvo_hi[:, :], wvo[:, :]).then_inc(wvo_hi_done, 1)

            split_w_hi(0)
            p_uT(0)
            act.wait_ge(wvo_ready, 1)
            act.copy(wvo[:, :], up_ps[0][:, 0:P]).then_inc(wvo_done, 1)
            act.wait_ge(params_in, 16)
            p_q(0)
            p_uT(1)
            p_values(0)
            p_exp(0, 0)
            p_exp(0, 1)
            p_q(1)
            p_attnT(0, 0)
            p_attnT(0, 1)
            split_w_hi(1)
            p_exp(1, 0)
            p_values(1)
            p_exp(1, 1)

            for j in range(PHASES):
                for n in range(UNITS):
                    if hi_on_act(j, n):
                        hi(j, n)
                    relu(j, n)
                    if j == 0:
                        if n in AT0_AT:
                            p_attnT(1, AT0_AT.index(n))
                        if n in AT0_LG:
                            p_gate_exp(AT0_LG.index(n))
                        if n in AT0_GT:
                            p_gatesT(AT0_GT.index(n))
                        if n == 20:
                            act.copy(wqk_hi[:, :, :].rearrange("p a h -> p (a h)"), wattn[:, 0:2 * P]
                                     ).then_inc(wqk_hi_done, 1)
                            split_wvo_hi()
                        if n in SPLIT_W_AT:
                            split_w_hi(SPLIT_W_AT.index(n) + 2)
                        if n == 24:
                            act.wait_ge(dcy_vec, 2)
                            act.activation(dcy[:, 3:4], dcy[:, 2:3], ACT.Exp, scale=-1.0).then_inc(dcy_act, 1)
                            act.wait_ge(dcy_act, 1)
                            act.activation(dcy[:, 4:5], dcy[:, 3:4], ACT.Ln, bias=1.0).then_inc(dcy_act, 1)
                        if n == 27:
                            act.wait_ge(dcy_vec, 4)
                            act.wait_ge(shapes_in, 16)
                            act.activation(dmask, dmask, ACT.Exp, scale=dcy[:, 6:7]).then_inc(dcy_act, 1)
                    if 1 <= j <= NCH and n == AT_VT:
                        r_qk(j - 1)
                    k = j + 1
                    if 2 <= k < PHASES:
                        if n == AT_UT:
                            p_uT(k)
                        if n == AT_UT + 1:
                            p_u_hi(k)
                        if n == AT_Q:
                            p_q(k)
                        if n == AT_K:
                            p_k(k)
                        if n in AT_SC:
                            p_exp(k, AT_SC.index(n))
                        if n in AT_AT:
                            p_attnT(k, AT_AT.index(n))
                        if n == AT_C:
                            p_context(k)
                        if n == AT_LG:
                            p_gate_exp(k)
                        if n == AT_GT:
                            p_gatesT(k)

        @block.vector
        def _(dve):
            def hi(j, n):
                T = UNITS * j + n
                if T >= NHS:
                    dve.wait_ge(down_ready, T - NHS + 1)
                dve.wait_ge(relu_done, T + 1)
                dve.tensor_copy(hhi[:, T % NHS, :], hF[:, T % NHF, :]).then_inc(hi_vec_done, 1)

            def lo(j, n):
                T = UNITS * j + n
                if T >= NHS:
                    dve.wait_ge(down_ready, T - NHS + 1)
                dve.wait_ge(relu_done, T + 1)
                dve.wait_ge(hi_act_done if hi_on_act(j, n) else hi_vec_done, hi_count(j, n, hi_on_act(j, n)))
                dve.tensor_tensor(hlo[:, T % NHS, :], hF[:, T % NHF, :], hhi[:, T % NHS, :].bitcast(F32),
                                  ALU.subtract).then_inc(lo_done, 1)

            def gate(j, e):
                G = NE * j + e
                dve.wait_ge(down_ready, UNITS * j + DQ * (e + 1))
                if j == 0 and e == 0:
                    dve.wait_ge(first_gates_in, 16)
                elif e == (FIRST_GATES if j == 0 else 0):
                    dve.wait_ge(gbc_in[j % 2], 16 * (j // 2 + 1))
                if G >= 2:
                    dve.wait_ge(sum_done, G - 1)
                dve.scalar_tensor_tensor(out=gated[:, e % 2, :], in0=down_ps[e % 2][:, :],
                                         scalar=pcol[:, COL_B2 + e:COL_B2 + e + 1],
                                         in1=gbc[:, j % 2, e, :], op0=ALU.add, op1=ALU.mult).then_inc(gate_done, 1)

            def norm_stats(chunk, count, st, mv, rs, stat, var, eps):
                for t in range(TL):
                    last = dve.bn_stats(st[:, t, :], row_tile(chunk, t))
                last.then_inc(stat, 1)
                dve.wait_ge(stat, count)
                for t in range(TL):
                    last = dve.bn_aggr(mv[:, t, :], st[:, t, :])
                last.then_inc(var, 1)
                dve.wait_ge(var, count)
                dve.tensor_scalar(rs[:, 0, :], mv[:, :, 1], EPS, None, ALU.add).then_inc(eps, 1)

            def norm_apply(chunk, count, dst, mv, rs, rstd, done):
                dve.wait_ge(rstd, count)
                for t in range(TL):
                    dve.tensor_scalar(dst[:, t, :], row_tile(chunk, t), mv[:, t, 0:1], rs[:, 1, t:t + 1],
                                      ALU.subtract, ALU.mult).then_inc(done, 1)

            def p_norm_stats(k):
                c = k % NCH
                if k == 2:
                    dve.wait_ge(xrest_in, 16)
                if k >= NCH:
                    dve.wait_ge(rx_done, c + 1)
                norm_stats(c, k + 1, st_p[:, k % 2], mv_p[:, k % 2], rs_p[:, k % 2], p_stat, p_var, p_eps)

            def p_norm(k):
                if k >= 3:
                    dve.wait_ge(u_lo_done, k - 2)
                norm_apply(k % NCH, k + 1, u_of(k), mv_p[:, k % 2], rs_p[:, k % 2], p_rstd, p_u)

            def p_uT_parts(k):
                dve.wait_ge(uT_done, k + 1)
                dve.tensor_copy(uT_hi[:, :], uT[:, :]).then_inc(uT_hi_done, 1)
                dve.wait_ge(uT_hi_done, k - 1)
                dve.tensor_tensor(uT_lo[:, :], uT[:, :], uT_hi[:, :].bitcast(F32), ALU.subtract).then_inc(uT_lo_done, 1)

            def p_q_lo(k):
                dve.wait_ge(q_done, k + 1)
                dve.scalar_tensor_tensor(out=qT_lo[:, :], in0=p_ps[1][:, :], scalar=pcol[:, COL_BQ:COL_BQ + 1],
                                         in1=qT_hi[:, :].bitcast(F32), op0=ALU.add, op1=ALU.subtract).then_inc(q_lo_done, 1)

            def p_k(k):
                dve.wait_ge(k_ready, k + 1)
                dve.tensor_scalar(kT_of(k), side_bank(k, 0)[:, :], pcol[:, COL_BK:COL_BK + 1], None, ALU.add
                                  ).then_inc(k_done, 1)

            def p_k_lo(k):
                dve.wait_ge(k_done, k + 1)
                dve.scalar_tensor_tensor(out=kT_lo[:, :], in0=p_ps[0][:, :], scalar=pcol[:, COL_BK:COL_BK + 1],
                                         in1=kT_hi[:, :].bitcast(F32), op0=ALU.add, op1=ALU.subtract).then_inc(k_lo_done, 1)

            def p_attnT_lo(k, b):
                dve.wait_ge(at_done, NB * k + b + 1)
                dve.tensor_tensor(attnT_lo[:, b, :, :].rearrange("p a s -> p (a s)"), p_ps[1 - b][:, :],
                                  attnT_hi[:, b, :, :].rearrange("p a s -> p (a s)").bitcast(F32),
                                  ALU.subtract).then_inc(at_lo_done, 1)

            def p_context_lo(k):
                dve.wait_ge(c_done, k - 1)
                dve.tensor_tensor(cT_lo[:, :], p_ps[1][:, :], cT_hi[:, :].bitcast(F32), ALU.subtract).then_inc(c_lo_done, 1)

            def p_max(k, b):
                dve.wait_ge(sc_ready, NB * k + b + 1)
                dve.tensor_reduce(smx[:, k % 2, b, :], side_bank(k, 1 - b)[:, :].rearrange("p (i s) -> p i s", i=2),
                                  AX_X, ALU.max).then_inc(smx_done, 1)
                dve.wait_ge(smx_done, NB * k + b + 1)
                dve.tensor_scalar(nmx[:, k % 2, b, :], smx[:, k % 2, b, :], -SCALE, None, ALU.mult).then_inc(nmx_done, 1)

            def p_attn(k, b):
                dve.wait_ge(exp_done, NB * k + b + 1)
                dve.reciprocal(rsum[:, k % 2, b, :], esum[:, k % 2, b, :]).then_inc(rsum_done, 1)
                dve.wait_ge(rsum_done, NB * k + b + 1)
                for i in range(2):
                    last = dve.tensor_scalar(ex_of(k)[:, b, i, :], ex_of(k)[:, b, i, :], rsum[:, k % 2, b, i:i + 1],
                                             None, ALU.mult)
                last.then_inc(attn_done, 1)

            def p_z(k):
                par = k % 2
                dve.wait_ge(a_ready, k + 1)
                if k == 0:
                    dve.wait_ge(bvo_done, 1)
                dve.scalar_tensor_tensor(out=facc[:, par, :], in0=side_bank(k, 1 if k < 2 else 0)[:, :], scalar=bvo[:, 0:1],
                                         in1=uT_of(k), op0=ALU.add, op1=ALU.add).then_inc(z_done, 1)
                dve.wait_ge(z_done, k + 1)
                dve.tensor_copy(zhi[:, par, :], facc[:, par, :]).then_inc(zhi_done, 1)

            def p_zlo(k):
                par = k % 2
                dve.wait_ge(zhi_done, k + 1)
                dve.tensor_tensor(zlo[:, par, :], facc[:, par, :], zhi[:, par, :].bitcast(F32),
                                  ALU.subtract).then_inc(zlo_done, 1)

            def p_gate_shift(k):
                dve.wait_ge(lg_ready, k + 1)
                dve.tensor_tensor(lg[:, :, :], p_ps[1][:, 0:TL * NE].rearrange("p (t e) -> p t e", t=TL),
                                  pcol[:, COL_BG:COL_BG + NE].unsqueeze(1).to_broadcast([P, TL, NE]), ALU.add).then_inc(lg_done, 1)
                dve.wait_ge(lg_done, k + 1)
                dve.tensor_reduce(lmx[:, :], lg[:, :, :], AX_X, ALU.max).then_inc(lmx_done, 1)
                dve.wait_ge(lmx_done, k + 1)
                dve.tensor_tensor(lsh[:, :, :], lg[:, :, :], lmx[:, :].unsqueeze(2).to_broadcast([P, TL, NE]),
                                  ALU.subtract).then_inc(lsh_done, 1)

            def p_gate_norm(k):
                dve.wait_ge(lex_done, k + 1)
                dve.tensor_reduce(lsm[:, :], lex[:, :, :], AX_X, ALU.add).then_inc(lsm_done, 1)
                dve.wait_ge(lsm_done, k + 1)
                dve.reciprocal(lrc[:, :], lsm[:, :]).then_inc(lrc_done, 1)
                dve.wait_ge(lrc_done, k + 1)
                dve.tensor_tensor(gts[:, :, :].rearrange("p e t -> p t e"), lex[:, :, :], lrc[:, :].unsqueeze(2).to_broadcast([P, TL, NE]),
                                  ALU.mult).then_inc(gts_done, 1)

            def fold(j):
                dve.wait_ge(fold_ready, j + 1)
                rows = rows_of(j % NCH)
                dve.scalar_tensor_tensor(out=rows, in0=r_ps[:, :].rearrange("p (t h) -> p t h", t=TL),
                                         scalar=0.5, in1=rows, op0=ALU.mult, op1=ALU.add).then_inc(fold_done, 1)

            def r_norm_stats(c):
                dve.wait_ge(fold_done, c + 1)
                norm_stats(c, c + 1, st_r, mv_r, rs_r, r_stat, r_var, r_eps)

            def r_norm(c):
                if c == 0:
                    dve.wait_ge(wlo_done, 2 * NE)
                norm_apply(c, c + 1, v, mv_r, rs_r, r_rstd, r_v)

            def r_decay(c, b):
                dve.wait_ge(rsc_ready, NB * c + b + 1)
                dve.wait_ge(dmask_done, 1)
                dve.tensor_tensor(pT[:, b, :], r_ps[:, 0:384], dmask, ALU.mult).then_inc(pT_done, 1)

            def r_add(c):
                dve.wait_ge(r_ready, c + 1)
                rows = rows_of(c)
                dve.scalar_tensor_tensor(out=rows, in0=r_ps[:, :].rearrange("p (t h) -> p t h", t=TL),
                                         scalar=pcol[:, COL_OSCALE:COL_OSCALE + 1], in1=rows, op0=ALU.mult, op1=ALU.add
                                         ).then_inc(rx_done, 1)

            dve.memset(hF[:, 0, 0:SEQ], 0.0).then_inc(warm_set, 1)
            dve.wait_ge(x0_in, 16)
            p_norm_stats(0)
            p_norm(0)
            dve.wait_ge(x1_in, 16)
            p_norm_stats(1)
            p_norm(1)
            dve.wait_ge(params_in, 16)
            p_k(0)
            p_max(0, 0)
            p_max(0, 1)
            p_attn(0, 0)
            p_attn(0, 1)
            dve.wait_ge(bvo_ready, 1)
            dve.tensor_tensor(bvo[:, :], down_ps[0][:, 0:1], pcol[:, COL_BO:COL_BO + 1], ALU.add).then_inc(bvo_done, 1)
            p_k(1)
            p_z(0)
            p_max(1, 0)
            p_zlo(0)
            p_max(1, 1)
            p_attn(1, 0)
            p_attn(1, 1)

            for j in range(PHASES):
                k = j + 1
                for n in range(UNITS):
                    if j == 0:
                        if n == AT0_C:
                            p_z(1)
                        if n == AT0_C + 1:
                            p_zlo(1)
                        if n in AT0_LG:
                            p_gate_shift(AT0_LG.index(n))
                        if n - 1 in AT0_LG:
                            p_gate_norm(AT0_LG.index(n - 1))
                    if j >= 1:
                        if n == AT_FOLD:
                            fold(j - 1)
                        if j <= NCH:
                            if n == AT_RNORM:
                                r_norm_stats(j - 1)
                            if n == AT_RNORM + 2:
                                r_norm(j - 1)
                            if n in AT_RSC:
                                r_decay(j - 1, AT_RSC.index(n))
                            if n == AT_R:
                                r_add(j - 1)
                    if 2 <= k < PHASES:
                        if n == AT_NORM:
                            p_norm_stats(k)
                        if n == AT_NORM + 2:
                            p_norm(k)
                        if n == AT_UT:
                            p_uT_parts(k)
                        if n == AT_Q:
                            p_q_lo(k)
                        if n == AT_K:
                            p_k_lo(k)
                        if n in AT_AT:
                            p_attnT_lo(k, AT_AT.index(n))
                        if n == AT_C:
                            p_context_lo(k)
                        if n in AT_SC:
                            p_max(k, AT_SC.index(n))
                        if n - 1 in AT_SC:
                            p_attn(k, AT_SC.index(n - 1))
                        if n == AT_A:
                            p_z(k)
                        if n == AT_A + 1:
                            p_zlo(k)
                        if n == AT_LG:
                            p_gate_shift(k)
                        if n == AT_LG + 1:
                            p_gate_norm(k)
                    if j == 0 and n == 16:
                        dve.tensor_scalar(dcy[:, 1:2], pcol[:, COL_DECAY:COL_DECAY + 1], -1.0, None, ALU.mult).then_inc(dcy_vec, 1)
                        dve.wait_ge(dcy_vec, 1)
                        dve.tensor_tensor(dcy[:, 2:3], pcol[:, COL_DECAY:COL_DECAY + 1], dcy[:, 1:2], ALU.max).then_inc(dcy_vec, 1)
                        dve.tensor_scalar(dcy[:, 5:6], pcol[:, COL_DECAY:COL_DECAY + 1], 0.0, None, ALU.min).then_inc(dcy_vec, 1)
                    if j == 0 and n == 26:
                        dve.wait_ge(dcy_act, 2)
                        dve.wait_ge(dcy_vec, 3)
                        dve.tensor_tensor(dcy[:, 6:7], dcy[:, 5:6], dcy[:, 4:5], ALU.subtract).then_inc(dcy_vec, 1)
                    if j == 0 and n == 29:
                        dve.wait_ge(dcy_act, 3)
                        dve.tensor_tensor(dmask, dmask, shp[:, 0, :], ALU.mult).then_inc(dmask_done, 1)
                    if j == PHASES - 1 and n == END_GATE:
                        gate(j, NE - 2)
                    if not hi_on_act(j, n):
                        hi(j, n)
                    lo(j, n)
                    m = n - LAG - 1
                    if j == PHASES - 1 and m // DQ == NE - 2:
                        continue
                    if m >= 0 and m % DQ == DQ - 1:
                        gate(j, m // DQ)
                    elif m < 0 and (m + UNITS) % DQ == DQ - 1 and j >= 1:
                        gate(j - 1, NE - 1)
            fold(PHASES - 1)
            e = NE - 1
            dve.wait_ge(down_ready, UNITS * PHASES)
            for b in range(NB):
                cols = slice(b * SEQ, (b + 1) * SEQ)
                dve.scalar_tensor_tensor(out=gated[:, e % 2, cols], in0=down_ps[e % 2][:, cols],
                                         scalar=pcol[:, COL_B2 + e:COL_B2 + e + 1],
                                         in1=gbc[:, (PHASES - 1) % 2, e, cols], op0=ALU.add, op1=ALU.mult
                                         ).then_inc(end_gate_done, 1)
            for b in range(NB):
                dve.wait_ge(end_fold_ready, b + 1)
                rows = xs[:, (NCH - 1) * TL + 2 * b:(NCH - 1) * TL + 2 * b + 2, :]
                dve.scalar_tensor_tensor(out=rows, in0=p_ps[b][:, 0:SEQ].rearrange("p (t h) -> p t h", t=2),
                                         scalar=0.5, in1=rows, op0=ALU.mult, op1=ALU.add).then_inc(end_fold_done, 1)

        @block.gpsimd
        def _(pool):
            def rstd(count, rs, eps, done):
                pool.wait_ge(eps, count)
                pool.tensor_tensor(rs[:, 1, :], rs[:, 0, :], mhalf[:, :], ALU.pow).then_inc(done, 1)

            def u_low(k):
                pool.wait_ge(u_hi_done, k - 1)
                pool.tensor_tensor(u_lo[:, :, :], u[:, :, :], u_hi[:, :, :].bitcast(F32), ALU.subtract
                                   ).then_inc(u_lo_done, 1)

            def split_w_lo(e):
                pool.wait_ge(whi_done, 2 * e + 1)
                pool.tensor_tensor(w1lo[:, e, :], wraw[:, e % NWR, 0, :], w1hi[:, e, :].bitcast(F32), ALU.subtract
                                   ).then_inc(wlo_done, 1)
                pool.wait_ge(whi_done, 2 * e + 2)
                pool.tensor_tensor(w2lo[:, e, :], wraw[:, e % NWR, 1, :], w2hi[:, e, :].bitcast(F32), ALU.subtract
                                   ).then_inc(wlo_done, 1)

            def add(j, e):
                G = NE * j + e
                pool.wait_ge(gate_done, G + 1)
                if G >= 1:
                    pool.wait_ge(sum_done, G)
                acc = facc[:, j % 2, :]
                pool.tensor_tensor(acc, acc, gated[:, e % 2, :], ALU.add).then_inc(sum_done, 1)

            pool.memset(mhalf[:, :], -0.5).then_inc(mhalf_set, 1)
            pool.wait_ge(mhalf_set, 1)
            for k in range(2):
                rstd(k + 1, rs_p[:, k], p_eps, p_rstd)
            split_w_lo(0)
            split_w_lo(1)
            for j in range(PHASES):
                if 2 <= j + 1 < PHASES:
                    rstd(j + 2, rs_p[:, (j + 1) % 2], p_eps, p_rstd)
                if j >= 1:
                    add(j - 1, NE - 1)
                    if j <= NCH:
                        rstd(j, rs_r, r_eps, r_rstd)
                for e in range(NE - 1):
                    if j == 0 and e + 2 < NE:
                        split_w_lo(e + 2)
                    if j == 0 and e == NE - 2:
                        pool.wait_ge(wqk_hi_done, 1)
                        pool.tensor_tensor(wqk_lo[:, :, :].rearrange("p a h -> p (a h)"), wattn[:, 0:2 * P],
                                           wqk_hi[:, :, :].rearrange("p a h -> p (a h)").bitcast(F32), ALU.subtract
                                           ).then_inc(wqk_lo_done, 1)
                        pool.wait_ge(wvo_hi_done, 1)
                        pool.tensor_tensor(wvo_lo[:, :], wvo[:, :], wvo_hi[:, :].bitcast(F32), ALU.subtract
                                           ).then_inc(wvo_lo_done, 1)
                    add(j, e)
                    if e == 0 and 2 <= j + 1 < PHASES:
                        u_low(j + 1)


SCALE = float(P) ** -0.5


def kernel(**inputs):
    import numpy as np
    import concourse.bacc as bacc
    from concourse.bass_utils import run_bass_kernel_spmd as run

    def ffn(name):
        return np.asarray(inputs["L0_ffn_" + name])

    def attn(name):
        return np.asarray(inputs["L0_attn_" + name])

    x = attn("x")
    x_rows = np.ascontiguousarray(x.reshape(-1, P, P).transpose(1, 0, 2))
    w1 = ffn("W1").transpose(1, 0, 2)
    w2 = ffn("W2").reshape(NE, DQ, P, P).transpose(2, 0, 1, 3).reshape(P, NE, CH)
    experts = np.ascontiguousarray(np.stack([w1, w2], axis=2))
    attn_weights = np.concatenate([ffn("Wq"), ffn("Wk"), ffn("Wv").T, ffn("Wo"), ffn("Wg")], axis=1)
    vectors = [ffn("b1").reshape(NE * DQ, P), ffn("b2")]
    vectors += [a.reshape(1, P) for a in (ffn("bq"), ffn("bk"), ffn("bv"), ffn("bo"),
                                          attn("q_scale"), attn("k_scale"))]
    everywhere = [attn("decay_logit").reshape(1), attn("out_scale").reshape(1), ffn("bg")]
    params = np.concatenate([np.concatenate(vectors).T,
                             np.broadcast_to(np.concatenate(everywhere), (P, 2 + NE))], axis=1)

    s = np.arange(P)[:, None]
    diff = np.concatenate([s - np.arange(P)[None, :], s + P - np.arange(SEQ)[None, :]], axis=1)
    decay_shapes = np.stack([diff > 0, np.maximum(diff - 1, 0)], axis=1).astype(np.float32)

    nc = bacc.Bacc("TRN2", target_bir_lowering=False, num_devices=1)
    arrays = {"x_rows": x_rows, "experts": experts, "attn_weights": attn_weights, "params": params,
              "identity": np.eye(P, dtype=np.float32), "decay_shapes": decay_shapes}
    arrays = {name: np.ascontiguousarray(a) for name, a in arrays.items()}
    args = [nc.dram_tensor(name, a.shape, mybir.dt.from_np(a.dtype), kind="ExternalInput").ap()
            for name, a in arrays.items()]
    args.append(nc.dram_tensor("gates_scratch", (2, NE, CH), F32, kind="Internal").ap())
    args.append(nc.dram_tensor("out_rows", x_rows.shape, F32, kind="ExternalOutput").ap())
    macaron(nc, *args)
    r = run(nc, [arrays], core_ids=[0])
    return r.results[0]["out_rows"].transpose(1, 0, 2).reshape(x.shape)
```
